# Optimizing a Trainium2 kernel written in Bass

```python
import numpy as np
import jax
import jax.numpy as jnp

def _softmax(x, axis=-1):
    return jax.nn.softmax(x, axis=axis)

def _gelu(x):
    return jax.nn.gelu(x, approximate=True)

def _silu(x):
    return jax.nn.silu(x)

def _sigmoid(x):
    return jax.nn.sigmoid(x)

def _layernorm(x, axis=-1, eps=1e-05):
    m = jnp.mean(x, axis=axis, keepdims=True)
    v = jnp.var(x, axis=axis, keepdims=True)
    return (x - m) / jnp.sqrt(v + eps)

def _scatter_add(tgt, idx, src, axis=0):
    return tgt.at[idx].add(src)

def _segment_sum(src, seg, n):
    return jax.ops.segment_sum(src, seg, n)
kernel_name = 'mk_recurrent_d2_jaxref_r8_0e2e03'

def setup_inputs(seed: int=0):
    np.random.seed(seed)
    _w = jnp.asarray

    def _L0_attn_setup():
        import jax, jax.numpy as jnp
        import numpy as np
        B, N, D, H = (8, 512, 128, 16)
        HD = D // H
        EPS = 1e-05
        key = jax.random.key(seed)
        ks = jax.random.split(key, 18)
        s = 1.0 / np.sqrt(D)

        def lin(k):
            return (jax.random.normal(k, (D, D), jnp.float32) * s, jnp.zeros((D,), jnp.float32))
        Wg_w, Wg_b = lin(ks[0])
        Wr_w, Wr_b = lin(ks[1])
        Wk_w, Wk_b = lin(ks[2])
        Wv_w, Wv_b = lin(ks[3])
        Wo_w, Wo_b = lin(ks[4])
        mg = jax.random.uniform(ks[5], (D,), jnp.float32)
        mr = jax.random.uniform(ks[6], (D,), jnp.float32)
        mk = jax.random.uniform(ks[7], (D,), jnp.float32)
        mv = jax.random.uniform(ks[8], (D,), jnp.float32)
        w = jax.random.normal(ks[9], (H, HD), jnp.float32)
        u = jax.random.normal(ks[10], (H, HD), jnp.float32)
        x = jax.random.normal(ks[11], (B, N, D), jnp.float32)
        return {'x': x, 'Wg_w': Wg_w, 'Wg_b': Wg_b, 'Wr_w': Wr_w, 'Wr_b': Wr_b, 'Wk_w': Wk_w, 'Wk_b': Wk_b, 'Wv_w': Wv_w, 'Wv_b': Wv_b, 'Wo_w': Wo_w, 'Wo_b': Wo_b, 'mg': mg, 'mr': mr, 'mk': mk, 'mv': mv, 'w': w, 'u': u}
    _L0_attn_in = _L0_attn_setup()

    def _L0_ffn_setup():
        import jax, jax.numpy as jnp
        import numpy as np
        HIDDEN = 128
        NUM_EXPERTS = 8
        TOP_K = 2
        B, S = (2, 256)
        key = jax.random.key(seed)
        k1, k2, k3, k4, k5 = jax.random.split(key, 5)
        d, dff, E = (HIDDEN, 4 * HIDDEN, NUM_EXPERTS)
        x = jax.random.normal(k1, (B, S, d), dtype=jnp.float32)
        W1 = jax.random.normal(k2, (E, d, dff), dtype=jnp.float32) * (1.0 / np.sqrt(d))
        b1 = jax.random.normal(k3, (E, dff), dtype=jnp.float32) * 0.01
        W2 = jax.random.normal(k4, (E, dff, d), dtype=jnp.float32) * (1.0 / np.sqrt(dff))
        b2 = jax.random.normal(k5, (E, d), dtype=jnp.float32) * 0.01
        return {'x': x, 'W1': W1, 'b1': b1, 'W2': W2, 'b2': b2}
    _L0_ffn_in = _L0_ffn_setup()

    def _L1_attn_setup():
        import jax, jax.numpy as jnp
        import numpy as np
        N_HEADS = 16
        SCALE = 8.0
        key = jax.random.key(seed)
        k1, k2, k3, k4 = jax.random.split(key, 4)
        b, n, d_model, inner = (8, 256, 128, 128)
        x = jax.random.normal(k1, (b, n, d_model), dtype=jnp.float32)
        Wqkv = jax.random.normal(k2, (3 * inner, d_model), dtype=jnp.float32) * (1.0 / np.sqrt(d_model))
        Wproj = jax.random.normal(k3, (d_model, inner), dtype=jnp.float32) * (1.0 / np.sqrt(inner))
        bproj = jax.random.normal(k4, (d_model,), dtype=jnp.float32) * 0.01
        return {'x': x, 'Wqkv': Wqkv, 'Wproj': Wproj, 'bproj': bproj}
    _L1_attn_in = _L1_attn_setup()

    def _L1_ffn_setup():
        import jax, jax.numpy as jnp
        import numpy as np
        B, S, D, O, E, K = (2, 256, 128, 128, 8, 2)
        key = jax.random.key(seed)
        ks = jax.random.split(key, 6)

        def w(k, shape, fan_in):
            return jax.random.normal(k, shape, jnp.float32) * fan_in ** (-0.5)
        return {'x': jax.random.normal(ks[0], (B, S, D), jnp.float32), 'gate_w': w(ks[1], (E, D), D), 'gate_b': jnp.zeros((E,), jnp.float32), 'w1': w(ks[2], (E, D, O), D), 'b1': jnp.zeros((E, O), jnp.float32), 'w2': w(ks[3], (E, O, O), O), 'b2': jnp.zeros((E, O), jnp.float32), 'w3': w(ks[4], (E, O, O), O), 'b3': jnp.zeros((E, O), jnp.float32)}
    _L1_ffn_in = _L1_ffn_setup()
    _d = {'L0_attn_x': _L0_attn_in['x'], 'L0_attn_Wg_w': _L0_attn_in['Wg_w'], 'L0_attn_Wg_b': _L0_attn_in['Wg_b'], 'L0_attn_Wr_w': _L0_attn_in['Wr_w'], 'L0_attn_Wr_b': _L0_attn_in['Wr_b'], 'L0_attn_Wk_w': _L0_attn_in['Wk_w'], 'L0_attn_Wk_b': _L0_attn_in['Wk_b'], 'L0_attn_Wv_w': _L0_attn_in['Wv_w'], 'L0_attn_Wv_b': _L0_attn_in['Wv_b'], 'L0_attn_Wo_w': _L0_attn_in['Wo_w'], 'L0_attn_Wo_b': _L0_attn_in['Wo_b'], 'L0_attn_mg': _L0_attn_in['mg'], 'L0_attn_mr': _L0_attn_in['mr'], 'L0_attn_mk': _L0_attn_in['mk'], 'L0_attn_mv': _L0_attn_in['mv'], 'L0_attn_w': _L0_attn_in['w'], 'L0_attn_u': _L0_attn_in['u'], 'L0_ffn_W1': _L0_ffn_in['W1'], 'L0_ffn_b1': _L0_ffn_in['b1'], 'L0_ffn_W2': _L0_ffn_in['W2'], 'L0_ffn_b2': _L0_ffn_in['b2'], 'L1_attn_Wqkv': _L1_attn_in['Wqkv'], 'L1_attn_Wproj': _L1_attn_in['Wproj'], 'L1_attn_bproj': _L1_attn_in['bproj'], 'L1_ffn_gate_w': _L1_ffn_in['gate_w'], 'L1_ffn_gate_b': _L1_ffn_in['gate_b'], 'L1_ffn_w1': _L1_ffn_in['w1'], 'L1_ffn_b1': _L1_ffn_in['b1'], 'L1_ffn_w2': _L1_ffn_in['w2'], 'L1_ffn_b2': _L1_ffn_in['b2'], 'L1_ffn_w3': _L1_ffn_in['w3'], 'L1_ffn_b3': _L1_ffn_in['b3']}
    _x0 = _d['L0_attn_x']
    _d['L0_attn_x'] = jax.random.normal(jax.random.fold_in(jax.random.key(seed), 1), (32, 256, 128), dtype=_x0.dtype)
    del _x0
    return _d

def reference(L0_attn_x, L0_attn_Wg_w, L0_attn_Wg_b, L0_attn_Wr_w, L0_attn_Wr_b, L0_attn_Wk_w, L0_attn_Wk_b, L0_attn_Wv_w, L0_attn_Wv_b, L0_attn_Wo_w, L0_attn_Wo_b, L0_attn_mg, L0_attn_mr, L0_attn_mk, L0_attn_mv, L0_attn_w, L0_attn_u, L0_ffn_W1, L0_ffn_b1, L0_ffn_W2, L0_ffn_b2, L1_attn_Wqkv, L1_attn_Wproj, L1_attn_bproj, L1_ffn_gate_w, L1_ffn_gate_b, L1_ffn_w1, L1_ffn_b1, L1_ffn_w2, L1_ffn_b2, L1_ffn_w3, L1_ffn_b3):

    def _L0_attn_ref(x, Wg_w, Wg_b, Wr_w, Wr_b, Wk_w, Wk_b, Wv_w, Wv_b, Wo_w, Wo_b, mg, mr, mk, mv, w, u):
        import jax, jax.numpy as jnp
        import numpy as np
        B, N, D, H = (8, 512, 128, 16)
        HD = D // H
        EPS = 1e-05
        b, n, d = x.shape
        x_shift = jnp.roll(x, shift=1, axis=1)

        def mix(m, W, bias):
            return (m * x + (1.0 - m) * x_shift) @ W.T + bias
        g = mix(mg, Wg_w, Wg_b).reshape(b, n, H, HD)
        r = mix(mr, Wr_w, Wr_b).reshape(b, n, H, HD)
        k = mix(mk, Wk_w, Wk_b).reshape(b, n, H, HD)
        v = mix(mv, Wv_w, Wv_b).reshape(b, n, H, HD)
        kv = k * v
        decay = jnp.exp(-jnp.exp(w))
        kv_t = jnp.swapaxes(kv, 0, 1)

        def step(acc, kvt):
            acc = decay * acc + kvt
            return (acc, acc)
        _, accs = jax.lax.scan(step, jnp.zeros((b, H, HD), x.dtype), kv_t)
        wkv = jnp.swapaxes(accs, 0, 1) + u * kv
        rw = r * wkv
        mean = jnp.mean(rw, axis=-1, keepdims=True)
        var = jnp.var(rw, axis=-1, keepdims=True)
        ln = (rw - mean) * jax.lax.rsqrt(var + EPS)
        out = (jax.nn.sigmoid(g) * ln).reshape(b, n, d)
        return out @ Wo_w.T + Wo_b

    def _L0_ffn_ref(x, W1, b1, W2, b2):
        import jax, jax.numpy as jnp
        import numpy as np
        HIDDEN = 128
        NUM_EXPERTS = 8
        TOP_K = 2
        B, S = (2, 256)
        Bm, Sm, d = x.shape
        E = W1.shape[0]
        x_flat = x.reshape(-1, d)
        h = jnp.mod(x_flat[:, :TOP_K].sum(axis=1).astype(jnp.int32), E)
        sel = jnp.stack([h, jnp.mod(h + 1, E)], axis=1)

        def step(acc, params):
            e, W1e, b1e, W2e, b2e = params
            w = jnp.any(sel == e, axis=1).astype(x.dtype) / TOP_K
            y = jnp.maximum(x_flat @ W1e + b1e, 0.0) @ W2e + b2e
            return (acc + w[:, None] * y, None)
        init = jnp.zeros_like(x_flat)
        out_flat, _ = jax.lax.scan(step, init, (jnp.arange(E), W1, b1, W2, b2))
        return out_flat.reshape(Bm, Sm, d)

    def _L1_attn_ref(x, Wqkv, Wproj, bproj):
        import jax, jax.numpy as jnp
        import numpy as np
        N_HEADS = 16
        SCALE = 8.0
        b, n, _ = x.shape
        qkv = jnp.einsum('bnm,fm->bnf', x, Wqkv)
        qkv = qkv.reshape(b, n, N_HEADS, -1)
        dh = qkv.shape[3] // 3
        q, k, v = (qkv[..., :dh], qkv[..., dh:2 * dh], qkv[..., 2 * dh:])
        scores = jnp.einsum('bnhd,bngd->bnhg', q, k) / SCALE
        attn = jax.nn.softmax(scores, axis=-1)
        out = jnp.einsum('bnhg,bngd->bnhd', attn, v)
        out = out.reshape(b, n, -1)
        return jnp.einsum('bni,mi->bnm', out, Wproj) + bproj

    def _L1_ffn_ref(x, gate_w, gate_b, w1, b1, w2, b2, w3, b3):
        import jax, jax.numpy as jnp
        import numpy as np
        B, S, D, O, E, K = (2, 256, 128, 128, 8, 2)
        probs = jax.nn.softmax(x @ gate_w.T + gate_b, axis=-1)
        _, topi = jax.lax.top_k(probs, K)
        onehot = jax.nn.one_hot(topi, E, dtype=probs.dtype)
        cw = jnp.einsum('bske,bsk->bse', onehot, probs[..., :K])
        out = jnp.zeros(x.shape[:2] + (O,), x.dtype)
        for e in range(E):
            h = jax.nn.relu(x @ w1[e] + b1[e])
            h = jax.nn.relu(h @ w2[e] + b2[e])
            h = h @ w3[e] + b3[e]
            out = out + cw[..., e:e + 1] * h
        return out
    x = L0_attn_x
    xn = _layernorm(x, axis=-1)
    s = _L0_attn_ref(xn, L0_attn_Wg_w, L0_attn_Wg_b, L0_attn_Wr_w, L0_attn_Wr_b, L0_attn_Wk_w, L0_attn_Wk_b, L0_attn_Wv_w, L0_attn_Wv_b, L0_attn_Wo_w, L0_attn_Wo_b, L0_attn_mg, L0_attn_mr, L0_attn_mk, L0_attn_mv, L0_attn_w, L0_attn_u)
    g = _silu(_L0_ffn_ref(xn, L0_ffn_W1, L0_ffn_b1, L0_ffn_W2, L0_ffn_b2))
    x = x + s * g
    xn = _layernorm(x, axis=-1)
    s = _L1_attn_ref(xn, L1_attn_Wqkv, L1_attn_Wproj, L1_attn_bproj)
    g = _silu(_L1_ffn_ref(xn, L1_ffn_gate_w, L1_ffn_gate_b, L1_ffn_w1, L1_ffn_b1, L1_ffn_w2, L1_ffn_b2, L1_ffn_w3, L1_ffn_b3))
    x = x + s * g
    return x

_drawn_inputs = setup_inputs


def setup_inputs(seed=0):
    import zlib

    import numpy as np

    out = dict(_drawn_inputs(seed))
    spreads = {'L0_attn_Wg_b': (0.0, 0.8),
     'L0_attn_Wr_b': (0.0, 0.292),
     'L0_attn_Wk_b': (0.0, 0.1),
     'L0_attn_Wv_b': (0.0, 0.299),
     'L0_attn_Wo_b': (0.0, 0.297),
     'L1_ffn_gate_b': (0.0, 0.8),
     'L1_ffn_b1': (0.0, 0.8),
     'L1_ffn_b2': (0.0, 0.8),
     'L1_ffn_b3': (0.0, 2.0)}
    factors = {'L0_ffn_b1': 8.0,
     'L0_ffn_b2': 8.0,
     'L1_attn_Wqkv': 3.469,
     'L1_attn_Wproj': 3.424,
     'L1_attn_bproj': 48.038,
     'L1_ffn_gate_w': 3.655,
     'L1_ffn_w1': 5.086,
     'L1_ffn_w2': 4.396,
     'L1_ffn_w3': 3.525}
    for name, (base, spread) in spreads.items():
        noise = np.random.default_rng([zlib.crc32(name.encode()), seed]).standard_normal(out[name].shape)
        drawn = base * np.exp(spread * noise) if base else spread * noise
        out[name] = jnp.asarray(drawn.astype(out[name].dtype))
    for name, factor in factors.items():
        out[name] = (out[name] * factor).astype(out[name].dtype)
    return out
```

```python
import concourse.bass as bass
from concourse import mybir
from contextlib import ExitStack

P = 128
TB = 4
NT = TB * P
SEQ = 256
NSEQ = NT // SEQ
H, HD = 16, 8
E = 8
FF = 512
FC = FF // P
EPS = 1e-5
C_MIX = 0
C_BR, C_BK, C_BV, C_U, C_W = 4, 5, 6, 7, 8
C_B1 = 9
C_LB1 = C_B1 + E * FC
C_LB2 = C_LB1 + E
NCOL = C_LB2 + E
G_, R_, K_, V_ = 0, 1, 2, 3


class Signal:

    def __init__(self, sem, per, start=0):
        self.sem, self.per, self.start = sem, per, start

    def at(self, i, n):
        return i * self.per + (n + self.start)


class Chain:

    def __init__(self, eng, sem):
        self.eng, self.sem, self.base, self.n, self.i, self.per = eng, sem, 0, 0, 0, 0

    def enter(self, i, per):
        self.base += self.n
        self.i, self.per, self.n = i, per, 0

    def leave(self, blocks):
        assert self.n == self.per, f"chain: {self.n} steps, not {self.per}"
        self.base += blocks * self.per
        self.i, self.per, self.n = 0, 0, 0

    def add(self, ins):
        ins.then_inc(self.sem, 1)
        self.n += 1
        return ins

    def wait(self):
        self.eng.wait_ge(self.sem, self.i * self.per + (self.base + self.n))

    def link(self, ins):
        self.add(ins)
        self.wait()


def two_layers(nc, x, w4, wo, w1, w2, wqkv, wproj, gate, l1, l2, l3, cols, rows, b2, b3, consts, out):
    fp = mybir.dt.float32
    i32 = mybir.dt.int32
    ALU = mybir.AluOpType
    ACT = mybir.ActivationFunctionType
    X = mybir.AxisListType.X

    ntok = x.shape[0]
    NTILE = ntok // P
    NB = ntok // NT

    ctx = ExitStack()
    with ctx:
        def sb(name, shape, dt=fp):
            return ctx.enter_context(nc.sbuf_tensor(name, shape, dt))

        def bank(name):
            return ctx.enter_context(nc.psum_tensor(name, [P, 512], fp))

        def sem(name):
            return ctx.enter_context(nc.semaphore(name))

        x_all = sb("x_all", [P, NTILE, P])
        s_sb = sb("s_sb", [P, NT])
        mv_all = sb("mv_all", [P, NTILE, 2])
        rstd_all = sb("rstd_all", [P, NTILE])
        w4_sb = sb("w4_sb", [P, 4, P])
        wo_sb = sb("wo_sb", [P, P])
        wqkv_sb = sb("wqkv_sb", [P, 3 * P])
        wproj_sb = sb("wproj_sb", [P, P])
        gate_sb = sb("gate_sb", [P, E])
        wts = sb("wts", [P, 2 * E * FC * P])
        w1_sb = wts[:, 0:E * FF].rearrange("p (e f) -> p e f", e=E)
        w2_sb = wts[:, E * FF:2 * E * FF].rearrange("p (e c d) -> p e c d", e=E, c=FC)
        l_sb = [sb(f"l{n}_sb", [P, E, P]) for n in (1, 2, 3)]
        cols_sb = sb("cols_sb", [P, NCOL])
        rows_sb = sb("rows_sb", [P, 3 * P + 3 * E])
        bo_bc, bg_bc, bp_bc = (rows_sb[:, n * P:(n + 1) * P] for n in range(3))
        gateb_bc = rows_sb[:, 3 * P:3 * P + E]
        iota = rows_sb[:, 3 * P + E:3 * P + 2 * E]
        rev = rows_sb[:, 3 * P + 2 * E:3 * P + 3 * E]
        b2_sb = sb("b2_sb", [E, P])
        b3_sb = sb("b3_sb", [E, P])
        ident = sb("ident", [P, P])
        center = sb("center", [P, P])
        decay = sb("decay", [P, SEQ])
        ew = sb("ew", [P, 2])
        ones = sb("ones", [P, SEQ])
        eps1 = sb("eps1", [P, 2])

        st_all = sb("st_all", [P, NTILE, 6])
        xn = sb("xn", [P, TB, P])
        xnT = sb("xnT", [P, NSEQ, SEQ + 1])
        xcur, xprev = xnT[:, :, 1:SEQ + 1], xnT[:, :, 0:SEQ]
        xn1 = xnT[:, :, :].rearrange("p b t -> p (b t)")[:, 0:NT]
        diff = sb("diff", [P, NSEQ, SEQ])
        mix = sb("mix", [P, 4, NT])
        v1 = sb("v1", [P, NT])
        kv = sb("kv", [P, NT])
        acc = sb("acc", [P, NT])
        wkv = sb("wkv", [P, NT])
        rw = sb("rw", [P, NT])
        gb = sb("gb", [P, NT])
        th = sb("th", [P, NT])
        sq = sb("sq", [P, NT])
        vs = sb("vs", [P, TB * H])
        sd = sb("sd", [P, TB * H])
        rh = sb("rh", [P, TB * H])
        t1 = sb("t1", [P, NT])
        o = sb("o", [P, NT])
        oT = sb("oT", [P, NT])
        cl = sb("cl", [P, 8, TB])
        cli = sb("cli", [P, 2, TB], i32)
        ew8 = sb("ew8", [P, 6, TB, E])
        wT = sb("wT", [E, NT])
        y = sb("y", [P, NT])
        th2 = sb("th2", [P, NT])
        hT = sb("hT", [P, 2, FC, NT])
        qkv = sb("qkv", [P, TB, 3 * P])
        prod = sb("prod", [P, H * H * HD])
        S = sb("S", [P, 2, H * H])
        A = sb("A", [P, 2, H * H])
        mx = sb("mx", [P, 2, H])
        den = sb("den", [P, TB * H])
        rden = sb("rden", [P, TB * H])
        av = hT[:, :, :, :].rearrange("p a c n -> p a (c n)")
        h1s = mix[:, 0:2, :]
        h2s = mix[:, 2:4, :]
        sm = sb("sm", [P, 4, TB])
        obuf = sb("obuf", [P, TB, P])

        bT, bK, bV, bR = bank("bT"), bank("bK"), bank("bV"), bank("bR")
        bH = [bank("bH0"), bank("bH1")]
        bY = [bank("bY0"), bank("bY1")]
        bQ = [bK, bV]
        bS = bR

        x_in, w_in, wb_in = sem("x_in"), sem("w_in"), sem("wb_in")
        out_done = sem("out_done")
        dve_own, act_own = sem("dve_own"), sem("act_own")
        var_ready, sd_ready, ones_ready, decay1_ready = sem("var_ready"), sem("sd_ready"), sem("ones_ready"), sem("decay1_ready")
        eps_ready = sem("eps_ready")
        sums_done, var2_ready, sd2_ready = sem("sums_done"), sem("var2_ready"), sem("sd2_ready")
        def signal(name, per, start=0):
            return Signal(sem(name), per, start)

        a_xn = signal("a_xn", 1)
        a_xT = signal("a_xT", 1)
        a_xnT = signal("a_xnT", 1)
        a_mix = signal("a_mix", 4)
        a_proj = signal("a_proj", 4)
        a_v = signal("a_v", 1)
        a_rw = signal("a_rw", 1)
        a_gb = signal("a_gb", 1)
        a_w = signal("a_w", 1)
        a_wTp = signal("a_wTp", 1)
        a_wT = signal("a_wT", 1)
        a_y0 = signal("a_y0", 1)
        a_yinit = signal("a_yinit", 1)
        a_c = signal("a_c", 1)
        a_sq = signal("a_sq", 1)
        a_vs = signal("a_vs", 1)
        a_sd = signal("a_sd", 1)
        a_o = signal("a_o", 1)
        a_oTp = signal("a_oTp", 1)
        a_oT = signal("a_oT", 1)
        a_s = signal("a_s", 1)
        a_h = signal("a_h", E * FC)
        a_hT = signal("a_hT", E * FC, 2)
        a_y = signal("a_y", E, 2)
        a_comb = signal("a_comb", E, 2)
        a_th2 = signal("a_th2", 1)
        b_xn = signal("b_xn", 1)
        b_xT = signal("b_xT", 1)
        b_xnT = signal("b_xnT", 1)
        b_lg = signal("b_lg", 1)
        b_lgs = signal("b_lgs", 1)
        b_ex = signal("b_ex", 1)
        b_cw = signal("b_cw", 1)
        b_cwTp = signal("b_cwTp", 1)
        b_cwT = signal("b_cwT", 1)
        b_y0 = signal("b_y0", 1)
        b_yinit = signal("b_yinit", 1)
        b_qkvp = signal("b_qkvp", TB)
        b_qkv = signal("b_qkv", TB, 2)
        b_sc = signal("b_sc", TB)
        b_a = signal("b_a", TB)
        b_av = signal("b_av", TB)
        b_avr = signal("b_avr", TB, 2)
        b_o = signal("b_o", 1)
        b_oTp = signal("b_oTp", 1)
        b_oT = signal("b_oT", 1)
        b_s = signal("b_s", 1)
        b_h = signal("b_h", 2 * E)
        b_hs = signal("b_hs", 2 * E, 2)
        b_y = signal("b_y", E)
        b_comb = signal("b_comb", E, 2)
        b_th = signal("b_th", 1)
        b_out = signal("b_out", 1)

        HID = [(1, 0)]
        for e in range(E):
            if e + 1 < E:
                HID.append((1, e + 1))
            HID.append((2, e))

        def tiles(i):
            return bass.ds(i * TB, TB)

        def tile_of(i, j):
            return bass.ds(i * TB + j, 1)

        def col(n):
            return cols_sb[:, n:n + 1]

        def byt(ap):
            return ap.rearrange("p (j d) -> p j d", j=TB)

        def bc(ap, shape):
            return ap.to_broadcast(shape)

        block = ctx.enter_context(nc.Block())

        NX = 4
        x_v = x.rearrange("(n p) d -> p n d", p=P)

        @block.sync
        def _(sp):
            n = NTILE // NX
            for c in range(NX):
                sp.dma_start(x_all[:, c * n:(c + 1) * n, :], x_v[:, c * n:(c + 1) * n, :]).then_inc(x_in, 16)
            sp.dma_start(cols_sb[:, :], cols).then_inc(w_in, 16)
            sp.dma_start(rows_sb[:, :], rows.partition_broadcast(P)).then_inc(w_in, 16)
            sp.dma_start(ident[:, :], consts[0]).then_inc(w_in, 16)
            sp.dma_start(center[:, :], consts[1]).then_inc(w_in, 16)
            sp.dma_start(w4_sb[:, :, :], w4).then_inc(w_in, 16)
            sp.dma_start(wo_sb[:, :], wo).then_inc(w_in, 16)
            sp.dma_start(w1_sb, w1.rearrange("e d f -> d e f")).then_inc(w_in, 16)
            sp.dma_start(w2_sb, w2.rearrange("e (c p) d -> p e c d", p=P)).then_inc(w_in, 16)
            sp.dma_start(b2_sb[:, :], b2).then_inc(w_in, 16)
            sp.dma_start(b3_sb[:, :], b3).then_inc(wb_in, 16)
            sp.dma_start(wqkv_sb[:, :], wqkv).then_inc(wb_in, 16)
            sp.dma_start(wproj_sb[:, :], wproj).then_inc(wb_in, 16)
            sp.dma_start(gate_sb[:, :], gate).then_inc(wb_in, 16)
            for n, lw in enumerate((l1, l2, l3)):
                sp.dma_start(l_sb[n][:, :, :], lw.rearrange("e d f -> d e f")).then_inc(wb_in, 16)
            out_v = out.rearrange("(n j p) d -> n p j d", j=TB, p=P)
            with sp.Fori(0, NB) as i:
                sp.wait_ge(b_out.sem, b_out.at(i, 1))
                sp.dma_start(out_v[bass.ds(i, 1)].rearrange("n p j d -> (n p) j d"), obuf[:, :, :]).then_inc(out_done, 16)
            sp.wait_ge(out_done, 16 * (NB + 1))

        W_ALL, WB_ALL = 16 * 9, 16 * 7

        @block.gpsimd
        def _(pool):
            pool.wait_ge(b_sc.sem, 1)
            with pool.Fori(0, NB) as i:
                for t in range(TB):
                    pool.wait_ge(b_a.sem, b_a.at(i, t + 1))
                    pool.wait_ge(b_avr.sem, b_avr.at(i, t - 1))
                    a_b = A[:, t % 2, :].rearrange("p (h g) -> p h g", h=H).unsqueeze(2).to_broadcast([P, H, HD, H])
                    v_b = qkv[:, t, :].rearrange("p (g c) -> p c g", c=3 * HD)[:, 2 * HD:3 * HD, :].unsqueeze(1).to_broadcast([P, H, HD, H])
                    nc.gpsimd.tensor_tensor(av[:, t % 2, :].rearrange("p (h d g) -> p h d g", h=H, d=HD), a_b, v_b, ALU.mult).then_inc(b_av.sem, 1)

        @block.scalar
        def _(act):
            act.wait_ge(w_in, W_ALL)
            nc.scalar.activation(ew[:, 0:1], col(C_W), ACT.Exp).then_inc(act_own, 1)
            act.wait_ge(act_own, 1)
            nc.scalar.activation(ew[:, 1:2], ew[:, 0:1], ACT.Exp, scale=-1.0).then_inc(decay1_ready, 1)
            act.sem_inc(a_hT.sem, 2)
            act.sem_inc(b_hs.sem, 2)
            act.sem_inc(b_qkv.sem, 2)
            act.wait_ge(var_ready, 1)
            nc.scalar.activation(rstd_all[:, :], mv_all[:, :, 1], ACT.Sqrt, bias=eps1[:, 0:1]).then_inc(sd_ready, 1)

            def relu_chunks(i, e):
                for c in range(FC):
                    k = e * FC + c
                    if c == 0:
                        act.wait_ge(a_y.sem, a_y.at(i, e - 1))
                    act.wait_ge(a_h.sem, a_h.at(i, k + 1))
                    nc.scalar.activation(hT[:, e % 2, c, :], bH[k % 2][:, :], ACT.Relu, bias=col(C_B1 + k)).then_inc(a_hT.sem, 1)

            with act.Fori(0, NB) as i:
                act.wait_ge(a_xT.sem, a_xT.at(i, 1))
                tp = bT[:, :].rearrange("p (b t) -> p b t", b=NSEQ)
                nc.scalar.activation(xcur, tp, ACT.Copy)
                nc.scalar.activation(xnT[:, :, 0:1], tp[:, :, SEQ - 1:SEQ], ACT.Copy).then_inc(a_xnT.sem, 1)
                relu_chunks(i, 0)
                act.wait_ge(a_proj.sem, a_proj.at(i, 1))
                nc.scalar.activation(v1[:, :], bV[:, :], ACT.Identity, bias=col(C_BV)).then_inc(a_v.sem, 1)
                act.wait_ge(a_wTp.sem, a_wTp.at(i, 1))
                nc.scalar.activation(wT[:, :], bV[0:E, :], ACT.Copy).then_inc(a_wT.sem, 1)
                act.wait_ge(a_y0.sem, a_y0.at(i, 1))
                nc.scalar.activation(y[:, :], bV[:, :], ACT.Copy).then_inc(a_yinit.sem, 1)
                relu_chunks(i, 1)
                act.wait_ge(a_gb.sem, a_gb.at(i, 1))
                nc.scalar.activation(th[:, :], gb[:, :], ACT.Tanh, scale=0.5)
                relu_chunks(i, 2)
                act.wait_ge(a_c.sem, a_c.at(i, 1))
                nc.scalar.activation(sq[:, :], bK[:, :], ACT.Square).then_inc(a_sq.sem, 1)
                act.wait_ge(a_vs.sem, a_vs.at(i, 1))
                nc.scalar.activation(sd[:, :], vs[:, :], ACT.Sqrt, bias=eps1[:, 1:2], scale=4.0 / HD).then_inc(a_sd.sem, 1)
                relu_chunks(i, 3)
                act.wait_ge(a_oTp.sem, a_oTp.at(i, 1))
                nc.scalar.activation(oT[:, :], bT[:, :], ACT.Copy).then_inc(a_oT.sem, 1)
                for e in range(4, E):
                    relu_chunks(i, e)
                act.wait_ge(a_comb.sem, a_comb.at(i, E))
                nc.scalar.activation(th2[:, :], y[:, :], ACT.Tanh, scale=0.5).then_inc(a_th2.sem, 1)

            act.wait_ge(var2_ready, 1)
            nc.scalar.activation(rstd_all[:, :], mv_all[:, :, 1], ACT.Sqrt, bias=eps1[:, 0:1]).then_inc(sd2_ready, 1)

            def relu_hidden(i, ks):
                for k in ks:
                    n, e = HID[k]
                    act.wait_ge(b_h.sem, b_h.at(i, k + 1))
                    nc.scalar.activation((h1s, h2s)[n - 1][:, e % 2, :], bH[k % 2][:, :], ACT.Relu,
                                         bias=col((C_LB1, C_LB2)[n - 1] + e)).then_inc(b_hs.sem, 1)

            def exps(i, t):
                act.wait_ge(b_sc.sem, b_sc.at(i, t + 1))
                nc.scalar.activation(A[:, t % 2, :], S[:, t % 2, :], ACT.Exp, scale=0.125).then_inc(b_a.sem, 1)

            with act.Fori(0, NB) as i:
                act.wait_ge(b_xT.sem, b_xT.at(i, 1))
                nc.scalar.activation(xn1, bT[:, :], ACT.Copy).then_inc(b_xnT.sem, 1)
                for t in range(TB):
                    act.wait_ge(b_qkvp.sem, b_qkvp.at(i, t + 1))
                    nc.scalar.activation(qkv[:, t, :], bQ[t % 2][:, 0:3 * P], ACT.Copy).then_inc(b_qkv.sem, 1)
                    if t == 1:
                        act.wait_ge(b_lgs.sem, b_lgs.at(i, 1))
                        nc.scalar.activation(ew8[:, 1], ew8[:, 0], ACT.Exp).then_inc(b_ex.sem, 1)
                relu_hidden(i, range(0, 3))
                exps(i, 0)
                act.wait_ge(b_cwTp.sem, b_cwTp.at(i, 1))
                nc.scalar.activation(wT[:, :], bS[0:E, :], ACT.Copy).then_inc(b_cwT.sem, 1)
                act.wait_ge(b_y0.sem, b_y0.at(i, 1))
                nc.scalar.activation(y[:, :], bS[:, :], ACT.Copy).then_inc(b_yinit.sem, 1)
                relu_hidden(i, range(3, 7))
                exps(i, 1)
                relu_hidden(i, range(7, 11))
                exps(i, 2)
                relu_hidden(i, range(11, 15))
                exps(i, 3)
                relu_hidden(i, range(15, 2 * E))
                act.wait_ge(b_comb.sem, b_comb.at(i, E))
                nc.scalar.activation(th2[:, :], y[:, :], ACT.Tanh, scale=0.5).then_inc(b_th.sem, 1)
                act.wait_ge(b_oTp.sem, b_oTp.at(i, 1))
                nc.scalar.activation(oT[:, :], bT[:, :], ACT.Copy).then_inc(b_oT.sem, 1)

        @block.vector
        def _(dve):
            own = Chain(dve, dve_own)
            link, add = own.link, own.add
            v = nc.vector
            dve.sem_inc(a_comb.sem, 2)
            dve.sem_inc(b_comb.sem, 2)
            dve.sem_inc(b_avr.sem, 2)
            v.memset(eps1[:, 0:1], EPS)
            v.memset(eps1[:, 1:2], 4 * EPS)
            link(v.memset(ones[:, :], 1.0))
            dve.wait_ge(decay1_ready, 1)
            v.tensor_scalar(decay[:, :], ones[:, :], ew[:, 1:2], None, ALU.mult)
            dve.wait_ge(x_in, 16 * NX)

            def stats(i):
                for j in range(TB):
                    last = v.bn_stats(st_all[:, tile_of(i, j), :], x_all[:, tile_of(i, j), :])
                link(last)

            def mean_var():
                me, qe, mo, qo = (st_all[:, :, n] for n in (1, 2, 4, 5))
                mean, var = mv_all[:, :, 0], mv_all[:, :, 1]
                link(v.tensor_tensor(mean, me, mo, ALU.subtract))
                link(v.scalar_tensor_tensor(var, mean, 0.25 * P, mean, ALU.mult, ALU.mult))
                link(v.tensor_tensor(var, var, qe, ALU.add))
                link(v.tensor_tensor(var, var, qo, ALU.add))
                link(v.tensor_scalar(var, var, 1.0 / P, None, ALU.mult))
                link(v.tensor_tensor(mean, me, mo, ALU.add))
                link(v.tensor_scalar(mean, mean, 0.5, None, ALU.mult))

            with dve.Fori(0, NB) as i:
                own.enter(i, 1)
                stats(i)
            own.leave(NB)
            mean_var()
            dve.sem_inc(var_ready, 1)
            dve.wait_ge(sd_ready, 1)
            link(v.reciprocal(rstd_all[:, :], rstd_all[:, :]))

            def normalise(i, ready):
                for j in range(TB):
                    t = tile_of(i, j)
                    last = v.tensor_scalar(xn[:, j, :], x_all[:, t, :], mv_all[:, t, 0], rstd_all[:, t],
                                           ALU.subtract, ALU.mult)
                last.then_inc(ready.sem, 1)
                return last

            def combine(i, e, comb, done, w):
                dve.wait_ge(done.sem, done.at(i, e + 1))
                for j in range(TB):
                    yj = y[:, j * P:(j + 1) * P]
                    last = v.scalar_tensor_tensor(yj, bY[e % 2][:, j * P:(j + 1) * P], w[:, j, e:e + 1], yj, ALU.mult, ALU.add)
                last.then_inc(comb.sem, 1)
                dve.wait_ge(comb.sem, comb.at(i, e + 1))

            def layer0(i):
                normalise(i, a_xn)
                dve.wait_ge(a_xn.sem, a_xn.at(i, 1))
                c_sum, c_abs, c_fl, c_gt, c_sg, c_t, c_0, c_1 = (cl[:, n, :] for n in range(8))
                link(v.tensor_tensor(c_sum, xn[:, :, 0], xn[:, :, 1], ALU.add))
                link(v.tensor_scalar(c_sg, c_sum, 0.0, None, ALU.is_ge))
                link(v.tensor_scalar(c_sg, c_sg, 2.0, -1.0, ALU.mult, ALU.add))
                link(v.tensor_tensor(c_abs, c_sum, c_sg, ALU.mult))
                link(v.tensor_copy(cli[:, 0, :], c_abs))
                link(v.tensor_copy(c_fl, cli[:, 0, :]))
                link(v.tensor_tensor(c_gt, c_fl, c_abs, ALU.is_gt))
                link(v.tensor_tensor(c_fl, c_fl, c_gt, ALU.subtract))
                link(v.tensor_tensor(cli[:, 0, :], c_fl, c_sg, ALU.mult))
                link(v.tensor_scalar(cli[:, 1, :], cli[:, 0, :], 7, None, ALU.bitwise_and))
                link(v.tensor_copy(c_0, cli[:, 1, :]))
                link(v.tensor_scalar(cli[:, 0, :], c_0, 1.0, None, ALU.add))
                link(v.tensor_scalar(cli[:, 1, :], cli[:, 0, :], 7, None, ALU.bitwise_and))
                link(v.tensor_copy(c_1, cli[:, 1, :]))
                io = iota.unsqueeze(1).to_broadcast([P, TB, E])
                link(v.tensor_tensor(ew8[:, 1], io, c_0.unsqueeze(2).to_broadcast([P, TB, E]), ALU.is_equal))
                link(v.tensor_tensor(ew8[:, 2], io, c_1.unsqueeze(2).to_broadcast([P, TB, E]), ALU.is_equal))
                link(v.tensor_tensor(ew8[:, 1], ew8[:, 1], ew8[:, 2], ALU.add))
                v.tensor_scalar(ew8[:, 0], ew8[:, 1], 0.5, None, ALU.mult).then_inc(a_w.sem, 1)
                dve.wait_ge(a_xnT.sem, a_xnT.at(i, 1))
                link(v.tensor_tensor(diff[:, :, :], xcur, xprev, ALU.subtract))
                for n in (V_, K_, R_, G_):
                    v.scalar_tensor_tensor(mix[:, n, :].rearrange("p (b t) -> p b t", b=NSEQ), diff[:, :, :],
                                           col(C_MIX + n), xprev, ALU.mult, ALU.add).then_inc(a_mix.sem, 1)
                dve.wait_ge(a_v.sem, a_v.at(i, 1))
                dve.wait_ge(a_proj.sem, a_proj.at(i, 2))
                link(v.scalar_tensor_tensor(kv[:, :], bK[:, :], col(C_BK), v1[:, :], ALU.add, ALU.mult))
                for b in range(NSEQ):
                    s_ = slice(b * SEQ, (b + 1) * SEQ)
                    last = v.tensor_tensor_scan(acc[:, s_], decay[:, :], kv[:, s_], 0.0, ALU.mult, ALU.add)
                link(last)
                link(v.scalar_tensor_tensor(wkv[:, :], kv[:, :], col(C_U), acc[:, :], ALU.mult, ALU.add))
                dve.wait_ge(a_proj.sem, a_proj.at(i, 3))
                v.scalar_tensor_tensor(rw[:, :], bR[:, :], col(C_BR), wkv[:, :], ALU.add, ALU.mult).then_inc(a_rw.sem, 1)
                dve.wait_ge(a_proj.sem, a_proj.at(i, 4))
                v.tensor_tensor(byt(gb[:, :]), byt(bT[:, :]), bg_bc.unsqueeze(1).to_broadcast([P, TB, P]), ALU.add).then_inc(a_gb.sem, 1)
                dve.wait_ge(a_yinit.sem, a_yinit.at(i, 1))
                combine(i, 0, a_comb, a_y, ew8[:, 0])
                combine(i, 1, a_comb, a_y, ew8[:, 0])
                dve.wait_ge(a_sq.sem, a_sq.at(i, 1))
                v.tensor_reduce(vs[:, :], sq[:, :].rearrange("p (h d) -> p h d", d=HD), X, ALU.add).then_inc(a_vs.sem, 1)
                link(v.scalar_tensor_tensor(t1[:, :], th[:, :], 1.0, bK[:, :], ALU.add, ALU.mult))
                dve.wait_ge(a_sd.sem, a_sd.at(i, 1))
                link(v.reciprocal(rh[:, :], sd[:, :]))
                v.tensor_tensor(o[:, :].rearrange("p (h d) -> p h d", d=HD), t1[:, :].rearrange("p (h d) -> p h d", d=HD),
                                rh[:, :].unsqueeze(2).to_broadcast([P, TB * H, HD]), ALU.mult).then_inc(a_o.sem, 1)
                combine(i, 2, a_comb, a_y, ew8[:, 0])
                combine(i, 3, a_comb, a_y, ew8[:, 0])
                combine(i, 4, a_comb, a_y, ew8[:, 0])
                dve.wait_ge(a_s.sem, a_s.at(i, 1))
                v.tensor_tensor(byt(s_sb[:, :]), byt(bR[:, :]), bo_bc.unsqueeze(1).to_broadcast([P, TB, P]), ALU.add)
                for e in range(5, E):
                    combine(i, e, a_comb, a_y, ew8[:, 0])
                dve.wait_ge(a_th2.sem, a_th2.at(i, 1))
                link(v.scalar_tensor_tensor(t1[:, :], th2[:, :], 1.0, y[:, :], ALU.add, ALU.mult))
                link(v.scalar_tensor_tensor(t1[:, :], s_sb[:, :], 0.5, t1[:, :], ALU.mult, ALU.mult))
                link(v.tensor_tensor(x_all[:, tiles(i), :], x_all[:, tiles(i), :], byt(t1[:, :]), ALU.add))

            dve.wait_ge(w_in, W_ALL)
            with dve.Fori(0, NB) as i:
                own.enter(i, 26)
                layer0(i)
            own.leave(NB)

            with dve.Fori(0, NB) as i:
                own.enter(i, 1)
                stats(i)
            own.leave(NB)
            mean_var()
            dve.sem_inc(var2_ready, 1)
            dve.wait_ge(sd2_ready, 1)
            link(v.reciprocal(rstd_all[:, :], rstd_all[:, :]))

            def scores(i, t):
                dve.wait_ge(b_qkv.sem, b_qkv.at(i, t + 1))
                heads = qkv[:, t, :].rearrange("p (h c) -> p h c", c=3 * HD)
                q_b = heads[:, :, 0:HD].unsqueeze(2).to_broadcast([P, H, H, HD])
                k_b = heads[:, :, HD:2 * HD].unsqueeze(1).to_broadcast([P, H, H, HD])
                link(v.tensor_tensor(prod[:, :].rearrange("p (h g d) -> p h g d", h=H, g=H), q_b, k_b, ALU.mult))
                s3 = S[:, t % 2, :].rearrange("p (h g) -> p h g", h=H)
                link(v.tensor_reduce(S[:, t % 2, :], prod[:, :].rearrange("p (s d) -> p s d", d=HD), X, ALU.add))
                link(v.tensor_reduce(mx[:, t % 2, :], s3, X, ALU.max))
                v.tensor_tensor(s3, s3, mx[:, t % 2, :].unsqueeze(2).to_broadcast([P, H, H]), ALU.subtract).then_inc(b_sc.sem, 1)

            def denominators(i, t):
                dve.wait_ge(b_a.sem, b_a.at(i, t + 1))
                add(v.tensor_reduce(den[:, t * H:(t + 1) * H], A[:, t % 2, :].rearrange("p (h g) -> p h g", h=H), X, ALU.add))

            def heads_out(i, t):
                dve.wait_ge(b_av.sem, b_av.at(i, t + 1))
                v.tensor_reduce(t1[:, t * P:(t + 1) * P], av[:, t % 2, :].rearrange("p (o g) -> p o g", g=H), X, ALU.add).then_inc(b_avr.sem, 1)

            def gating(i):
                lg, ex, pr, oh, sc, cw = (ew8[:, n] for n in (0, 1, 2, 3, 4, 5))
                m_, r_, z_, z2 = (sm[:, n, :] for n in range(4))
                b_ = lambda a: a.unsqueeze(2).to_broadcast([P, TB, E])
                rv = rev.unsqueeze(1).to_broadcast([P, TB, E])
                dve.wait_ge(b_lg.sem, b_lg.at(i, 1))
                link(v.tensor_tensor(lg, bS[:, 0:TB * E].rearrange("p (j e) -> p j e", j=TB),
                                     gateb_bc.unsqueeze(1).to_broadcast([P, TB, E]), ALU.add))
                link(v.tensor_reduce(m_, lg, X, ALU.max))
                v.tensor_tensor(lg, lg, b_(m_), ALU.subtract).then_inc(b_lgs.sem, 1)
                dve.wait_ge(b_ex.sem, b_ex.at(i, 1))
                link(v.tensor_reduce(z_, ex, X, ALU.add))
                link(v.reciprocal(z2, z_))
                link(v.tensor_tensor(pr, ex, b_(z2), ALU.mult))
                link(v.tensor_reduce(m_, pr, X, ALU.max))
                link(v.tensor_tensor(oh, pr, b_(m_), ALU.is_equal))
                link(v.tensor_tensor(sc, oh, rv, ALU.mult))
                link(v.tensor_reduce(r_, sc, X, ALU.max))
                link(v.tensor_tensor(oh, rv, b_(r_), ALU.is_equal))
                link(v.tensor_tensor(cw, oh, b_(pr[:, :, 0]), ALU.mult))
                link(v.scalar_tensor_tensor(ex, oh, -2.0, pr, ALU.mult, ALU.add))
                link(v.tensor_reduce(m_, ex, X, ALU.max))
                link(v.tensor_tensor(oh, ex, b_(m_), ALU.is_equal))
                link(v.tensor_tensor(sc, oh, rv, ALU.mult))
                link(v.tensor_reduce(r_, sc, X, ALU.max))
                link(v.tensor_tensor(oh, rv, b_(r_), ALU.is_equal))
                link(v.tensor_tensor(oh, oh, b_(pr[:, :, 1]), ALU.mult))
                v.tensor_tensor(cw, cw, oh, ALU.add).then_inc(b_cw.sem, 1)
                dve.wait_ge(b_cw.sem, b_cw.at(i, 1))

            def layer1(i):
                normalise(i, b_xn)
                gating(i)
                for t in range(TB):
                    scores(i, t)
                    if t:
                        heads_out(i, t - 1)
                    if t == 0:
                        dve.wait_ge(b_yinit.sem, b_yinit.at(i, 1))
                    combine(i, 2 * t, b_comb, b_y, ew8[:, 5])
                    combine(i, 2 * t + 1, b_comb, b_y, ew8[:, 5])
                    denominators(i, t)
                own.wait()
                link(v.reciprocal(rden[:, :], den[:, :]))
                heads_out(i, TB - 1)
                dve.wait_ge(b_avr.sem, b_avr.at(i, TB))
                v.tensor_tensor(o[:, :].rearrange("p (h d) -> p h d", d=HD), t1[:, :].rearrange("p (h d) -> p h d", d=HD),
                                rden[:, :].unsqueeze(2).to_broadcast([P, TB * H, HD]), ALU.mult).then_inc(b_o.sem, 1)
                dve.wait_ge(b_th.sem, b_th.at(i, 1))
                link(v.scalar_tensor_tensor(th2[:, :], th2[:, :], 1.0, y[:, :], ALU.add, ALU.mult))
                dve.wait_ge(b_s.sem, b_s.at(i, 1))
                link(v.tensor_tensor(byt(gb[:, :]), byt(bS[:, :]), bp_bc.unsqueeze(1).to_broadcast([P, TB, P]), ALU.add))
                link(v.scalar_tensor_tensor(gb[:, :], gb[:, :], 0.5, th2[:, :], ALU.mult, ALU.mult))
                dve.wait_ge(out_done, i * 16 + 16)
                v.tensor_tensor(obuf[:, :, :], byt(gb[:, :]), x_all[:, tiles(i), :], ALU.add).then_inc(b_out.sem, 1)

            dve.sem_inc(out_done, 16)
            with dve.Fori(0, NB) as i:
                own.enter(i, 18 + 4 * TB + 4)
                layer1(i)
            own.leave(NB)

        @block.tensor
        def _(pe):
            mm = nc.tensor.matmul
            pe.sem_inc(a_y.sem, 2)

            def tr(src, done, i):
                for j in range(TB):
                    last = nc.tensor.transpose(bT[:, j * P:(j + 1) * P], src[:, j * P:(j + 1) * P], ident[:, :])
                last.then_inc(done.sem, 1)

            def token_major(dst, src, rhs, done):
                for j in range(TB):
                    last = mm(dst[:, j * P:(j + 1) * P], src[:, j * P:(j + 1) * P], rhs, start=True, stop=True)
                last.then_inc(done.sem, 1)

            def small_transposes(dst, w, done):
                for j in range(TB):
                    last = nc.tensor.transpose(dst[0:E, j * P:(j + 1) * P], w[:, j, :], ident[:, :])
                last.then_inc(done.sem, 1)

            def hidden0(i, e):
                for c in range(FC):
                    k = e * FC + c
                    pe.wait_ge(a_hT.sem, a_hT.at(i, k - 1))
                    mm(bH[k % 2][:, :].rearrange("p (b t) -> p b t", b=NSEQ), w1_sb[:, e, c * P:(c + 1) * P], xcur, start=True, stop=True).then_inc(a_h.sem, 1)

            def out0(i, e):
                pe.wait_ge(a_hT.sem, a_hT.at(i, e * FC + FC))
                pe.wait_ge(a_comb.sem, a_comb.at(i, e - 1))
                for j in range(TB):
                    for c in range(FC):
                        last = mm(bY[e % 2][:, j * P:(j + 1) * P], hT[:, e % 2, c, j * P:(j + 1) * P], w2_sb[:, e, c, :],
                                  start=(c == 0), stop=(c == FC - 1))
                last.then_inc(a_y.sem, 1)

            pe.wait_ge(w_in, W_ALL)
            with pe.Fori(0, NB) as i:
                pe.wait_ge(a_xn.sem, a_xn.at(i, 1))
                tr(xn[:, :, :].rearrange("p j d -> p (j d)"), a_xT, i)
                pe.wait_ge(a_xnT.sem, a_xnT.at(i, 1))
                hidden0(i, 0)
                for n, (m, dst) in enumerate(((V_, bV), (K_, bK), (R_, bR))):
                    pe.wait_ge(a_mix.sem, a_mix.at(i, n + 1))
                    mm(dst[:, :], w4_sb[:, m, :], mix[:, m, :], start=True, stop=True).then_inc(a_proj.sem, 1)
                pe.wait_ge(a_mix.sem, a_mix.at(i, 4))
                token_major(bT, mix[:, G_, :], w4_sb[:, G_, :], a_proj)
                pe.wait_ge(a_w.sem, a_w.at(i, 1))
                pe.wait_ge(a_v.sem, a_v.at(i, 1))
                small_transposes(bV, ew8[:, 0], a_wTp)
                out0(i, 0)
                pe.wait_ge(a_wT.sem, a_wT.at(i, 1))
                token_major(bV, wT, b2_sb[:, :], a_y0)
                hidden0(i, 1)
                out0(i, 1)
                hidden0(i, 2)
                pe.wait_ge(a_rw.sem, a_rw.at(i, 1))
                token_major(bK, rw, center[:, :], a_c)
                out0(i, 2)
                hidden0(i, 3)
                out0(i, 3)
                pe.wait_ge(a_o.sem, a_o.at(i, 1))
                tr(o, a_oTp, i)
                hidden0(i, 4)
                out0(i, 4)
                pe.wait_ge(a_oT.sem, a_oT.at(i, 1))
                token_major(bR, oT, wo_sb[:, :], a_s)
                for e in range(5, E):
                    hidden0(i, e)
                    out0(i, e)

            def hidden1(i, k):
                n, e = HID[k]
                if n == 2:
                    pe.wait_ge(b_hs.sem, b_hs.at(i, HID.index((1, e)) + 1))
                pe.wait_ge(b_hs.sem, b_hs.at(i, k - 1))
                mm(bH[k % 2][:, :], l_sb[n - 1][:, e, :], xn1 if n == 1 else h1s[:, e % 2, :], start=True, stop=True).then_inc(b_h.sem, 1)

            def out1(i, e):
                pe.wait_ge(b_hs.sem, b_hs.at(i, HID.index((2, e)) + 1))
                pe.wait_ge(b_comb.sem, b_comb.at(i, e - 1))
                token_major(bY[e % 2], h2s[:, e % 2, :], l_sb[2][:, e, :], b_y)

            pe.wait_ge(wb_in, WB_ALL)
            with pe.Fori(0, NB) as i:
                pe.wait_ge(b_xn.sem, b_xn.at(i, 1))
                tr(xn[:, :, :].rearrange("p j d -> p (j d)"), b_xT, i)
                pe.wait_ge(b_xnT.sem, b_xnT.at(i, 1))
                for j in range(TB):
                    last = mm(bS[:, j * E:(j + 1) * E], xn1[:, j * P:(j + 1) * P], gate_sb[:, :], start=True, stop=True)
                last.then_inc(b_lg.sem, 1)
                for t in range(TB):
                    pe.wait_ge(b_qkv.sem, b_qkv.at(i, t - 1))
                    mm(bQ[t % 2][:, 0:3 * P], xn1[:, t * P:(t + 1) * P], wqkv_sb[:, :], start=True, stop=True).then_inc(b_qkvp.sem, 1)
                hidden1(i, 0)
                hidden1(i, 1)
                hidden1(i, 2)
                pe.wait_ge(b_cw.sem, b_cw.at(i, 1))
                small_transposes(bS, ew8[:, 5], b_cwTp)
                pe.wait_ge(b_cwT.sem, b_cwT.at(i, 1))
                token_major(bS, wT, b3_sb[:, :], b_y0)
                out1(i, 0)
                for k in range(3, 2 * E):
                    hidden1(i, k)
                    if HID[k][0] == 2:
                        out1(i, HID[k][1])
                pe.wait_ge(b_o.sem, b_o.at(i, 1))
                tr(o, b_oTp, i)
                pe.wait_ge(b_oT.sem, b_oT.at(i, 1))
                token_major(bS, oT, wproj_sb[:, :], b_s)


def kernel(**inputs):
    import numpy as _np
    import concourse.bacc as _bacc
    from concourse import mybir as _mybir
    from concourse.bass_utils import run_bass_kernel_spmd as _run

    a = {k: _np.asarray(v) for k, v in inputs.items()}
    x = a["L0_attn_x"]
    c = _np.ascontiguousarray
    names = ["mg", "mr", "mk", "mv", "Wr_b", "Wk_b", "Wv_b"]
    cols = [a["L0_attn_" + n].reshape(P) for n in names] + [a["L0_attn_u"].reshape(P), a["L0_attn_w"].reshape(P)]
    cols += list(a["L0_ffn_b1"].reshape(E * FC, P)) + list(a["L1_ffn_b1"]) + list(a["L1_ffn_b2"])
    idx = _np.arange(P)
    same_head = (idx[:, None] // HD == idx[None, :] // HD).astype(_np.float32)
    eye = _np.eye(P, dtype=_np.float32)
    steps = _np.arange(E, dtype=_np.float32)
    arrays = {
        "x": c(x.reshape(-1, P)),
        "w4": c(_np.stack([a[f"L0_attn_W{n}_w"].T for n in "grkv"], axis=1)),
        "wo": c(a["L0_attn_Wo_w"].T),
        "w1": c(a["L0_ffn_W1"]),
        "w2": c(a["L0_ffn_W2"]),
        "wqkv": c(a["L1_attn_Wqkv"].T),
        "wproj": c(a["L1_attn_Wproj"].T),
        "gate": c(a["L1_ffn_gate_w"].T),
        "l1": c(a["L1_ffn_w1"]), "l2": c(a["L1_ffn_w2"]), "l3": c(a["L1_ffn_w3"]),
        "cols": c(_np.stack(cols, axis=1)),
        "rows": c(_np.concatenate([a["L0_attn_Wo_b"], a["L0_attn_Wg_b"], a["L1_attn_bproj"], a["L1_ffn_gate_b"], steps, E - steps])),
        "b2": c(a["L0_ffn_b2"]), "b3": c(a["L1_ffn_b3"]),
        "consts": _np.stack([eye, eye - same_head / HD]).astype(_np.float32),
    }
    nc = _bacc.Bacc("TRN2", target_bir_lowering=False, num_devices=1)
    args = [nc.dram_tensor("in_" + n, v.shape, _mybir.dt.from_np(v.dtype), kind="ExternalInput").ap() for n, v in arrays.items()]
    out = nc.dram_tensor("out_0", arrays["x"].shape, _mybir.dt.float32, kind="ExternalOutput").ap()
    two_layers(nc, *args, out)
    r = _run(nc, [{"in_" + n: v for n, v in arrays.items()}], core_ids=[0])
    return r.results[0]["out_0"].reshape(x.shape)
```

```python
import concourse.bass as bass
from concourse import mybir
from contextlib import ExitStack

P = 128
TB = 4
NT = TB * P
SEQ = 256
NSEQ = NT // SEQ
H, HD = 16, 8
E = 8
FF = 512
FC = FF // P
EPS = 1e-5
C_MIX = 0
C_BR, C_BK, C_BV, C_U, C_W = 4, 5, 6, 7, 8
C_LB1 = 9
C_LB2 = C_LB1 + E
C_BG = C_LB2 + E
NCOL = C_BG + 1
PE_AV = (0, 2)
G_, R_, K_, V_ = 0, 1, 2, 3
MIXED = (R_, G_)
RW = P + 1
NU = 6


class Signal:

    def __init__(self, sem, per, start=0):
        self.sem, self.per, self.start = sem, per, start

    def at(self, i, n):
        return i * self.per + (n + self.start)


class Chain:

    def __init__(self, eng, sem):
        self.eng, self.sem, self.base, self.n, self.i, self.per, self.first = eng, sem, 0, 0, 0, 0, 0

    def enter(self, i, per, start=0):
        self.base += self.n
        self.first = start * per
        self.i, self.per, self.n = i, per, 0

    def leave(self, blocks):
        assert self.n == self.per, f"chain: {self.n} steps, not {self.per}"
        self.base += blocks * self.per
        self.i, self.per, self.n, self.first = 0, 0, 0, 0

    def add(self, ins):
        ins.then_inc(self.sem, 1)
        self.n += 1
        return ins

    def link(self, ins):
        self.add(ins)
        self.eng.wait_ge(self.sem, self.i * self.per + (self.base + self.n - self.first))


def two_layers(nc, x, w4, wo, w1b, w2, wqkv, wproj, gate, l1, l2, l3, cols, rows, b2, b3, consts, out):
    fp = mybir.dt.float32
    i32 = mybir.dt.int32
    ALU = mybir.AluOpType
    ACT = mybir.ActivationFunctionType
    X = mybir.AxisListType.X

    ntok = x.shape[0]
    NTILE = ntok // P
    NB = ntok // NT
    NTL = -(-(NTILE + E - 1) // NU) * NU
    NONE = 1 << 24
    WB = FF + FC

    xs = nc.dram_tensor("xs", [NTL * P, RW], fp).ap()
    gs = nc.dram_tensor("gs", [ntok, P], fp).ap()

    ctx = ExitStack()
    with ctx:
        def sb(name, shape, dt=fp):
            return ctx.enter_context(nc.sbuf_tensor(name, shape, dt))

        def bank(name):
            return ctx.enter_context(nc.psum_tensor(name, [P, 512], fp))

        def sem(name):
            return ctx.enter_context(nc.semaphore(name))

        def signal(name, per=1, start=0):
            return Signal(sem(name), per, start)

        x_all = sb("x_all", [P, NTILE, P])
        s_all = sb("s_all", [P, NTILE, P])
        st_all = sb("st_all", [P, NTILE, 6])
        mv_all = sb("mv_all", [P, NTILE, 2])
        rstd_all = sb("rstd_all", [P, NTILE])
        pos_i = sb("pos_i", [P, NTILE], i32)
        tid = sb("tid", [P, NTILE], i32)
        tcls = sb("tcls", [P, NTL], i32)
        w4_sb = sb("w4_sb", [P, 4, P])
        wm = sb("wm", [P, 4, 2, P])
        wo_sb = sb("wo_sb", [P, P])
        wqkv_sb = sb("wqkv_sb", [P, 3 * P])
        wproj_sb = sb("wproj_sb", [P, P])
        gate_sb = sb("gate_sb", [P, E])
        wts = sb("wts", [P, (E + 1) * WB + (E + 1) * FF])
        w1x = wts[:, 0:(E + 1) * WB].rearrange("p (e f) -> p e f", e=E + 1)
        w2x = wts[:, (E + 1) * WB:(E + 1) * (WB + FF)].rearrange("p (e c d) -> p e c d", e=E + 1, c=FC)
        g_all = wts[:, 0:ntok].rearrange("p (n d) -> p n d", d=P)
        l_sb = [sb(f"l{n}_sb", [P, E, P]) for n in (1, 2, 3)]
        cols_sb = sb("cols_sb", [P, NCOL])
        omm = sb("omm", [P, 4])
        hbg = sb("hbg", [P, 1])
        rows_sb = sb("rows_sb", [P, 2 * P + 3 * E + NTL])
        bo_bc, bp_bc = (rows_sb[:, n * P:(n + 1) * P] for n in range(2))
        gateb_bc = rows_sb[:, 2 * P:2 * P + E]
        iota = rows_sb[:, 2 * P + E:2 * P + 2 * E]
        rev = rows_sb[:, 2 * P + 2 * E:2 * P + 3 * E]
        tile_no = rows_sb[:, 2 * P + 3 * E:2 * P + 3 * E + NTL]
        b2_bc = sb("b2_bc", [P, E + 1, P])
        b2p = sb("b2p", [P, E, P])
        b3_sb = sb("b3_sb", [E, P])
        ident = sb("ident", [P, P])
        center = sb("center", [P, P])
        below = sb("below", [P, P])
        decay = sb("decay", [P, SEQ])
        ew = sb("ew", [P, 2])
        ones = sb("ones", [P, SEQ])
        eps1 = sb("eps1", [P, 2])

        WORK = 16384
        work = sb("work", [P, WORK])
        used = [0]

        def part(n):
            used[0] += n
            assert used[0] <= WORK
            return work[:, used[0] - n:used[0]]

        def lay(ap, pat, **kw):
            return ap.rearrange(pat, **kw)

        banks = [bank(f"bank{n}") for n in range(8)]

        used[0] = 0
        cls = [part(NTILE) for _ in range(8)]
        clsi = [part(NTILE).bitcast(i32) for _ in range(2)]
        x01 = lay(part(2 * NTILE), "p (n a) -> p n a", a=2)
        onehot = part(NTILE * E)
        oh3 = lay(onehot, "p (n c) -> p n c", c=E)
        cum = lay(part(NTILE * E), "p (c n) -> p c n", c=E)
        off = lay(part(NTILE * E), "p (n c) -> p n c", c=E)
        ncl = [part(E) for _ in range(4)]
        ncli = part(E).bitcast(i32)
        tcmp = lay(part(NTL * E), "p (k c) -> p k c", c=E)
        tcf = part(NTL)
        posf = part(NTILE)
        used[0] = 9 * NT + 3 * TB * H
        fill = lay(part(9 * RW), "p (a r) -> p a r", r=RW)
        xnrow = [lay(part(TB * RW), "p (j r) -> p j r", j=TB) for _ in range(2)]
        idx = [part(TB).bitcast(i32) for _ in range(2)]
        xnT = [lay(part(NSEQ * (SEQ + 1)), "p (b t) -> p b t", b=NSEQ) for _ in range(2)]
        th = [part(NT) for _ in range(2)]
        mix = {m: [part(NT) for _ in range(2)] for m in MIXED}
        diff = part(NT)
        used[0] = 0
        v1, kv, acc, wkv, rw, sq, o, oT = (part(NT) for _ in range(8))
        vs, sd, rh = (part(TB * H) for _ in range(3))
        used[0] = 0
        xsb = [part(RW) for _ in range(NU)]
        gout = [part(P) for _ in range(NU)]
        xsT = [part(P) for _ in range(2)]
        wc = [lay(part(2 * WB), "p (e f) -> p e f", e=2) for _ in range(2)]
        hs = [lay(part(2 * FF), "p (n t) -> p n t", t=P) for _ in range(2)]
        ye = [part(P) for _ in range(2)]
        the = [part(P) for _ in range(2)]
        used[0] = 0
        xn1 = lay(part(NT), "p (j d) -> p j d", j=TB)
        xT = [part(NT) for _ in range(2)]
        kvs = lay(part(TB * 2 * P), "p (j h c) -> p j h c", j=TB, h=H)
        prod = part(H * H * HD)
        av = [part(H * H * HD) for _ in range(2)]
        S = [part(H * H) for _ in range(2)]
        A = [part(H * H) for _ in range(2)]
        mx = [part(H) for _ in range(2)]
        den, rden = part(TB * H), part(TB * H)
        red = part(P)
        o1, oT1, th1, gy = (part(NT) for _ in range(4))
        y = [part(NT) for _ in range(2)]
        ysc = [part(NT) for _ in range(2)]
        h1s = [part(NT) for _ in range(2)]
        gw = [lay(part(TB * E), "p (j e) -> p j e", j=TB) for _ in range(5)]
        cw_ = [lay(part(TB * E), "p (j e) -> p j e", j=TB) for _ in range(2)]
        sm = [part(TB) for _ in range(4)]
        nmr_all, hbp = part(NTILE), part(P)
        h2s = [wts[:, n * NT:(n + 1) * NT] for n in range(2)]
        obuf = lay(wts[:, 2 * NT:3 * NT], "p (j d) -> p j d", j=TB)
        wT = wts[0:E, 3 * NT:4 * NT]
        fin, sp1 = (wts[:, n * NT:(n + 1) * NT] for n in (4, 5))

        x_in = [sem(f"x_in{c}") for c in range(4)]
        w_in, wb_in, fill_done = sem("w_in"), sem("wb_in"), sem("fill_done")
        we_in = sem("we_in")
        out_done = sem("out_done")
        dve_own, act_own = sem("dve_own"), sem("act_own")
        pool_turn = sem("pool_turn")
        consts_ready, w_decay, var_ready, sd_ready = sem("consts_ready"), sem("w_decay"), sem("var_ready"), sem("sd_ready")
        fill_ready, tid_ready, onehot_ready, counts_done, wm_ready = (sem(n) for n in ("fill_ready", "tid_ready", "onehot_ready", "counts_done", "wm_ready"))
        route_ready = sem("route_ready")
        g_in = [sem(f"g_in{c}") for c in range(4)]
        norm_ready = sem("norm_ready")
        sg_ready, x1_ready, var2_ready, sd2_ready = sem("sg_ready"), sem("x1_ready"), sem("var2_ready"), sem("sd2_ready")
        a_xn = signal("a_xn")
        a_scat = [sem(f"a_scat{p}") for p in range(2)]
        a_xT = signal("a_xT")
        a_xnT = signal("a_xnT")
        a_d = signal("a_d")
        a_mix = signal("a_mix")
        a_proj = signal("a_proj", 4)
        a_v = signal("a_v")
        a_rw = signal("a_rw")
        a_th = signal("a_th")
        a_c = signal("a_c")
        a_sq = signal("a_sq")
        a_vs = signal("a_vs")
        a_sd = signal("a_sd")
        a_o = signal("a_o")
        a_oTp = signal("a_oTp")
        a_oT = signal("a_oT")
        a_s = signal("a_s")
        a_se = signal("a_se", 1, 1)
        a_bo = signal("a_bo")
        e_ld = [sem(f"e_ld{u}") for u in range(NU)]
        e_sc = [sem(f"e_sc{u}") for u in range(NU)]
        e_wc = signal("e_wc")
        e_T = signal("e_T")
        e_xs = signal("e_xs")
        e_h = signal("e_h", 2)
        e_r0 = signal("e_r0")
        e_r1 = signal("e_r1")
        e_y = signal("e_y")
        e_yv = signal("e_yv", 1, 2)
        e_th = signal("e_th")
        e_g = signal("e_g")
        b_xn = signal("b_xn")
        b_xT = signal("b_xT")
        b_xq = signal("b_xq")
        b_lg = signal("b_lg")
        b_lgs = signal("b_lgs")
        b_ex = signal("b_ex")
        b_cw = signal("b_cw")
        b_cwTp = signal("b_cwTp")
        b_cwT = signal("b_cwT")
        b_y0 = signal("b_y0")
        b_yi = signal("b_yi")
        b_qkvp = signal("b_qkvp", TB)
        b_kv = signal("b_kv", TB)
        b_qk = signal("b_qk", TB)
        b_sc = signal("b_sc", TB)
        b_a = signal("b_a", TB)
        b_av = signal("b_av", TB)
        b_avp = signal("b_avp", max(1, len(PE_AV)))
        b_avr = signal("b_avr", max(1, TB - len(PE_AV)))
        b_of = signal("b_of", TB)
        b_oTp = signal("b_oTp")
        b_oT = signal("b_oT")
        b_s = signal("b_s")
        b_h = signal("b_h", 2 * E)
        b_hs = signal("b_hs", 2 * E, 2)
        b_y = signal("b_y", E)
        b_ys = signal("b_ys", E, 1)
        b_ya = signal("b_ya", E, 2)
        b_th = signal("b_th")
        b_gy = signal("b_gy")
        b_sp = signal("b_sp")
        b_sb = signal("b_sb")
        b_fin = signal("b_fin", 1, 1)
        b_out = signal("b_out")

        def hid(n, e, edge=False):
            if n == 1:
                return 1 if edge else 2 * e
            return 2 * e + 3 - edge

        def tiles(i):
            return bass.ds(i * TB, TB)

        def tile_of(i, j):
            return bass.ds(i * TB + j, 1)

        def col(n):
            return cols_sb[:, n:n + 1]

        def byt(ap):
            return ap.rearrange("p (j d) -> p j d", j=TB)

        def byseq(ap):
            return ap.rearrange("p (b t) -> p b t", b=NSEQ)

        def av_summed(t):
            pe = [u for u in range(TB) if u in PE_AV]
            no = [u for u in range(TB) if u not in PE_AV]
            return (b_avp, pe.index(t) + 1) if t in pe else (b_avr, no.index(t) + 1)

        block = ctx.enter_context(nc.Block())

        NX = 4
        CH = NTILE // NX
        x_v = x.rearrange("(n p) d -> p n d", p=P)
        g_v = gs.rearrange("(n p) d -> p n d", p=P)
        xs_v = xs.rearrange("(k p) r -> k p r", p=P)
        NI = NTL // NU
        W_ALL, WB_ALL, WE_ALL = 16 * 8, 16 * 7, 16 * 3

        @block.sync
        def _(sp):
            for c in range(NX):
                sp.dma_start(x_all[:, c * CH:(c + 1) * CH, :], x_v[:, c * CH:(c + 1) * CH, :]).then_inc(x_in[c], 16)
            sp.dma_start(rows_sb[:, :], rows.partition_broadcast(P)).then_inc(w_in, 16)
            sp.dma_start(cols_sb[:, :], cols).then_inc(w_in, 16)
            for n, m in enumerate((ident, center, below)):
                sp.dma_start(m[:, :], consts[n]).then_inc(w_in, 16)
            sp.dma_start(w4_sb[:, :, :], w4).then_inc(w_in, 16)
            sp.dma_start(wo_sb[:, :], wo).then_inc(w_in, 16)
            sp.dma_start(b2_bc[:, :, :], b2.rearrange("e d -> (e d)").partition_broadcast(P).rearrange("p (e d) -> p e d", e=E + 1)).then_inc(w_in, 16)
            sp.wait_ge(fill_ready, 1)
            for n in range(NTL // 9):
                sp.dma_start(xs_v[n * 9:(n + 1) * 9].rearrange("k p r -> p k r"), fill).then_inc(fill_done, 16)
            sp.dma_start(w1x, w1b.rearrange("e d f -> d e f")).then_inc(we_in, 16)
            sp.dma_start(w2x[:, 0:E], w2.rearrange("e (c p) d -> p e c d", p=P)).then_inc(we_in, 16)
            sp.dma_start(w2x[:, E], w2[0].rearrange("(c p) d -> p c d", p=P)).then_inc(we_in, 16)
            sp.dma_start(b3_sb[:, :], b3).then_inc(wb_in, 16)
            sp.dma_start(wqkv_sb[:, :], wqkv).then_inc(wb_in, 16)
            sp.dma_start(wproj_sb[:, :], wproj).then_inc(wb_in, 16)
            sp.dma_start(gate_sb[:, :], gate).then_inc(wb_in, 16)
            for n, lw in enumerate((l1, l2, l3)):
                sp.dma_start(l_sb[n][:, :, :], lw.rearrange("e d f -> d e f")).then_inc(wb_in, 16)

            for p in range(2):
                sp.wait_ge(a_scat[p], NB // 2 * 16 * TB)
            sp.wait_ge(a_se.sem, a_se.at(NB, 0))
            for u in range(NU):
                sp.dma_start(xsb[u], xs_v[u]).then_inc(e_ld[u], 16)
            with sp.Fori(1, NI) as i:
                for u in range(NU):
                    sp.wait_ge(e_sc[u], i * 16)
                    sp.dma_start(xsb[u], xs_v[bass.ds(i * NU + u, 1)].rearrange("k p r -> (k p) r")).then_inc(e_ld[u], 16)
            for u in range(NU):
                sp.wait_ge(e_sc[u], NI * 16)
            for c in range(NX):
                sp.dma_start(g_all[:, c * CH:(c + 1) * CH, :], g_v[:, c * CH:(c + 1) * CH, :]).then_inc(g_in[c], 16)

            out_v = out.rearrange("(n j p) d -> n p j d", j=TB, p=P)
            with sp.Fori(0, NB) as i:
                sp.wait_ge(b_out.sem, b_out.at(i, 1))
                sp.dma_start(out_v[bass.ds(i, 1)].rearrange("n p j d -> (n p) j d"), obuf[:, :, :]).then_inc(out_done, 16)
            sp.wait_ge(out_done, 16 * (NB + 1))

        @block.gpsimd
        def _(pool):
            pool.sem_inc(b_ya.sem, 2)
            pool.sem_inc(b_fin.sem, 1)
            pool.sem_inc(out_done, 16)
            nc.gpsimd.memset(fill, 0.0)
            nc.gpsimd.iota(tid[:, :], pattern=[[P, NTILE]], base=0, channel_multiplier=1).then_inc(tid_ready, 1)
            nc.gpsimd.drain()
            nc.gpsimd.memset(fill[:, :, P:RW].bitcast(i32), NONE).then_inc(fill_ready, 1)
            pool.wait_ge(fill_done, 16 * (NTL // 9))

            def scatter(n, p):
                pool.wait_ge(a_xn.sem, a_xn.at(n, 1))
                pool.sem_inc(pool_turn, 1)
                for j in range(TB):
                    nc.gpsimd.indirect_dma_start(xs, bass.IndirectOffsetOnAxis(idx[p][:, j:j + 1], 0), xnrow[p][:, j, :], None).then_inc(a_scat[p], 16)

            def add_bias(n):
                pool.wait_ge(a_se.sem, a_se.at(n, 1))
                nc.gpsimd.tensor_tensor(s_all[:, tiles(n), :], s_all[:, tiles(n), :], bo_bc.unsqueeze(1).to_broadcast([P, TB, P]), ALU.add).then_inc(a_bo.sem, 1)

            def differences(n, p, first=False):
                pool.wait_ge(a_xnT.sem, a_xnT.at(n, 1))
                if not first:
                    pool.wait_ge(a_mix.sem, a_mix.at(n, 0))
                nc.gpsimd.tensor_tensor(byseq(diff), xnT[p][:, :, 1:SEQ + 1], xnT[p][:, :, 0:SEQ], ALU.subtract).then_inc(a_d.sem, 1)

            differences(0, 0, first=True)
            scatter(0, 0)
            differences(1, 1)
            scatter(1, 1)
            scatter(2, 0)
            differences(2, 0)
            scatter(3, 1)
            with pool.Fori(0, (NB - 4) // 2) as r:
                for p in (1, 0):
                    i = r * 2 + (2 - p)
                    differences(i + 2, p)
                    scatter(i + 3, 1 - p)
                    add_bias(i - 1)
            differences(NB - 1, 1)
            for n in range(NB - 4, NB):
                add_bias(n)

            with pool.Fori(0, NI) as i:
                for u in range(NU):
                    pool.wait_ge(e_g.sem, e_g.at(i * NU + u, 1))
                    pool.sem_inc(pool_turn, 1)
                    nc.gpsimd.indirect_dma_start(gs, bass.IndirectOffsetOnAxis(xsb[u][:, P:RW].bitcast(i32), 0), gout[u], None,
                                                 bounds_check=ntok - 1, oob_is_err=False).then_inc(e_sc[u], 16)

            for c in range(NX):
                pool.wait_ge(sg_ready, c + 1)
                c_ = slice(c * CH, (c + 1) * CH)
                nc.gpsimd.tensor_tensor(x_all[:, c_, :], x_all[:, c_, :], s_all[:, c_, :], ALU.add).then_inc(x1_ready, 1)

            def weigh_v(i, t, first):
                pool.wait_ge(b_a.sem, b_a.at(i, t + 1))
                s_, n = av_summed((t + 2) % TB)
                if t >= 2:
                    pool.wait_ge(s_.sem, s_.at(i, n))
                elif not first:
                    pool.wait_ge(s_.sem, s_.at(i, n - s_.per))
                a_b = A[t % 2].rearrange("p (h g) -> p g h", h=H).unsqueeze(3).to_broadcast([P, H, H, HD])
                v_b = kvs[:, t, :, HD:2 * HD].unsqueeze(2).to_broadcast([P, H, H, HD])
                nc.gpsimd.tensor_tensor(av[t % 2].rearrange("p (g h d) -> p g h d", g=H, h=H), a_b, v_b, ALU.mult).then_inc(b_av.sem, 1)

            def add_expert(i, p, e):
                if e == 0:
                    pool.wait_ge(b_yi.sem, b_yi.at(i, 1))
                else:
                    pool.wait_ge(b_ya.sem, b_ya.at(i, e))
                pool.wait_ge(b_ys.sem, b_ys.at(i, e + 1))
                nc.gpsimd.tensor_tensor(y[p], y[p], ysc[e % 2], ALU.add).then_inc(b_ya.sem, 1)

            def add_x(i):
                pool.wait_ge(b_sp.sem, b_sp.at(i, 1))
                nc.gpsimd.tensor_tensor(byt(sp1), byt(sp1), hbp.unsqueeze(1).to_broadcast([P, TB, P]), ALU.add).then_inc(b_sb.sem, 1)
                pool.wait_ge(b_sb.sem, b_sb.at(i, 1))
                pool.wait_ge(b_gy.sem, b_gy.at(i, 1))
                nc.gpsimd.tensor_tensor(fin, sp1, gy, ALU.mult).then_inc(b_fin.sem, 1)
                pool.wait_ge(b_fin.sem, b_fin.at(i, 1))
                pool.wait_ge(out_done, i * 16 + 16)
                nc.gpsimd.tensor_tensor(obuf[:, :, :], byt(fin), x_all[:, tiles(i), :], ALU.add).then_inc(b_out.sem, 1)

            def layer1(i, p, first=False):
                if not first:
                    add_expert(i - 1, 1 - p, 7)
                weigh_v(i, 0, first)
                add_expert(i, p, 0)
                for t in range(1, TB):
                    add_expert(i, p, 2 * t - 1)
                    weigh_v(i, t, first)
                    add_expert(i, p, 2 * t)
                if not first:
                    add_x(i - 1)

            layer1(0, 0, first=True)
            with pool.Fori(0, (NB - 2) // 2) as r:
                layer1(r * 2 + 1, 1)
                layer1(r * 2 + 2, 0)
            layer1(NB - 1, 1)
            add_expert(NB - 1, 1, 7)
            add_x(NB - 1)

        @block.scalar
        def _(act):
            av_ = nc.scalar.activation
            act.wait_ge(w_in, W_ALL)
            av_(ew[:, 0:1], col(C_W), ACT.Exp).then_inc(act_own, 1)
            act.wait_ge(act_own, 1)
            av_(ew[:, 1:2], ew[:, 0:1], ACT.Exp, scale=-1.0).then_inc(w_decay, 1)
            act.sem_inc(a_se.sem, 1)
            act.sem_inc(b_hs.sem, 2)
            act.sem_inc(b_ys.sem, 1)
            act.wait_ge(var_ready, 1)
            av_(rstd_all[:, :], mv_all[:, :, 1], ACT.Sqrt, bias=eps1[:, 0:1]).then_inc(sd_ready, 1)

            def copy_xnT(n, p):
                act.wait_ge(a_xT.sem, a_xT.at(n, 1))
                tp = banks[0][:, :].rearrange("p (b t) -> p b t", b=NSEQ)
                av_(xnT[p][:, :, 1:SEQ + 1], tp, ACT.Copy)
                av_(xnT[p][:, :, 0:1], tp[:, :, SEQ - 1:SEQ], ACT.Copy).then_inc(a_xnT.sem, 1)

            def values0(n):
                act.wait_ge(a_proj.sem, a_proj.at(n, 1))
                av_(v1, banks[1][:, :], ACT.Identity, bias=col(C_BV)).then_inc(a_v.sem, 1)

            def gate0(n, p):
                act.wait_ge(a_proj.sem, a_proj.at(n, 4))
                av_(th[p], banks[4][:, :], ACT.Tanh, bias=hbg[:, :], scale=0.5).then_inc(a_th.sem, 1)

            def out0(n):
                act.wait_ge(a_s.sem, a_s.at(n, 1))
                av_(s_all[:, tiles(n), :], byt(banks[6][:, :]), ACT.Copy).then_inc(a_se.sem, 1)

            def block0(i, p, first=False, left=3):
                if left >= 2:
                    copy_xnT(i + 2, p)
                act.wait_ge(a_c.sem, a_c.at(i, 1))
                av_(sq, banks[5][:, :], ACT.Square).then_inc(a_sq.sem, 1)
                act.wait_ge(a_vs.sem, a_vs.at(i, 1))
                av_(sd, vs, ACT.Sqrt, bias=eps1[:, 1:2], scale=4.0 / HD).then_inc(a_sd.sem, 1)
                if left >= 1:
                    values0(i + 1)
                if not first:
                    out0(i - 1)
                if left >= 1:
                    gate0(i + 1, 1 - p)

            act.wait_ge(route_ready, 1)
            copy_xnT(0, 0)
            copy_xnT(1, 1)
            values0(0)
            gate0(0, 0)
            block0(0, 0, first=True)
            with act.Fori(0, (NB - 4) // 2) as r:
                for p in (1, 0):
                    block0(r * 2 + (2 - p), p)
            for n in range(NB - 3, NB):
                block0(n, n % 2, left=NB - 1 - n)
            out0(NB - 1)

            def rows_T(k, b):
                act.wait_ge(e_T.sem, e_T.at(k, 1))
                av_(xsT[b], banks[0][:, b * P:(b + 1) * P], ACT.Copy).then_inc(e_xs.sem, 1)

            def tile0(k, u, first=False, last=False):
                b = u % 2
                act.wait_ge(e_h.sem, e_h.at(k, 1))
                for c in range(FC):
                    r = av_(hs[b][:, c, :], banks[2 + 2 * b][:, c * P:(c + 1) * P], ACT.Relu, bias=wc[b][:, 0, FF + c:FF + c + 1])
                r.then_inc(e_r0.sem, 1)
                if not last:
                    rows_T(k + 2, b)
                if not first:
                    act.wait_ge(e_yv.sem, e_yv.at(k - 1, 1))
                    av_(the[1 - b], ye[1 - b], ACT.Tanh, scale=0.5).then_inc(e_th.sem, 1)

            rows_T(0, 0)
            rows_T(1, 1)
            for u in range(NU):
                tile0(u, u, first=(u == 0))
            with act.Fori(1, NI - 1) as i:
                for u in range(NU):
                    tile0(i * NU + u, u)
            for u in range(NU):
                tile0(NTL - NU + u, u, last=(u >= NU - 2))
            act.wait_ge(e_yv.sem, e_yv.at(NTL - 1, 1))
            av_(the[1], ye[1], ACT.Tanh, scale=0.5).then_inc(e_th.sem, 1)

            act.wait_ge(var2_ready, 1)
            av_(rstd_all[:, :], mv_all[:, :, 1], ACT.Sqrt, bias=eps1[:, 0:1]).then_inc(sd2_ready, 1)

            def normalise1(i, first=False):
                if not first:
                    act.wait_ge(b_xT.sem, b_xT.at(i, 0))
                for j in range(TB):
                    t = tile_of(i, j)
                    r = av_(xn1[:, j, :], x_all[:, t, :], ACT.Identity, scale=rstd_all[:, t], bias=nmr_all[:, t])
                r.then_inc(b_xn.sem, 1)

            def copy_sp(i):
                act.wait_ge(b_s.sem, b_s.at(i, 1))
                act.wait_ge(b_fin.sem, b_fin.at(i, 0))
                av_(sp1, banks[3][:, :], ACT.Copy, scale=0.5).then_inc(b_sp.sem, 1)

            def relu_hidden(i, n, e, edge=False):
                k = hid(n, e, edge)
                act.wait_ge(b_h.sem, b_h.at(i, k))
                av_((h1s, h2s)[n - 1][e % 2][:, :], banks[4 + k % 2][:, :], ACT.Relu,
                    bias=col((C_LB1, C_LB2)[n - 1] + e)).then_inc(b_hs.sem, 1)

            def weigh_expert(i, p, e):
                act.wait_ge(b_y.sem, b_y.at(i, e + 1))
                act.wait_ge(b_ya.sem, b_ya.at(i, e - 1))
                for j in range(TB):
                    r = av_(ysc[e % 2][:, j * P:(j + 1) * P], banks[6][:, j * P:(j + 1) * P], ACT.Copy, scale=cw_[p][:, j, e:e + 1])
                r.then_inc(b_ys.sem, 1)

            def hidden_step(i, e, last=False):
                if e < E - 1:
                    relu_hidden(i, 1, e + 1)
                elif not last:
                    relu_hidden(i + 1, 1, 0)
                relu_hidden(i, 2, e, last)

            def expert_step(i, p, e, first=False, last=False):
                hidden_step(i, e, last)
                if e:
                    weigh_expert(i, p, e - 1)
                elif not first:
                    weigh_expert(i - 1, 1 - p, E - 1)

            def exps(i, t):
                act.wait_ge(b_sc.sem, b_sc.at(i, t + 1))
                av_(A[t % 2], S[t % 2], ACT.Exp, scale=0.125).then_inc(b_a.sem, 1)

            def copy_kv(i, t, first):
                act.wait_ge(b_qkvp.sem, b_qkvp.at(i, t + 1))
                if not first:
                    act.wait_ge(b_av.sem, b_av.at(i, t + 1 - TB))
                av_(kvs[:, t], banks[1 + t % 2][:, 0:3 * P].rearrange("p (h c) -> p h c", h=H)[:, :, HD:3 * HD], ACT.Copy).then_inc(b_kv.sem, 1)

            def copy_xT(i, p):
                act.wait_ge(b_xT.sem, b_xT.at(i, 1))
                av_(xT[p], banks[0][:, :], ACT.Copy).then_inc(b_xq.sem, 1)

            def copy_oT(i):
                act.wait_ge(b_oTp.sem, b_oTp.at(i, 1))
                av_(oT1, banks[0][:, :], ACT.Copy).then_inc(b_oT.sem, 1)

            def tanh1(i, p):
                act.wait_ge(b_ya.sem, b_ya.at(i, E))
                av_(th1, y[p], ACT.Tanh, scale=0.5).then_inc(b_th.sem, 1)

            def start_y(i, p):
                act.wait_ge(b_y0.sem, b_y0.at(i, 1))
                av_(y[p], banks[3][:, :], ACT.Copy).then_inc(b_yi.sem, 1)

            def copy_wT(i):
                act.wait_ge(b_cwTp.sem, b_cwTp.at(i, 1))
                av_(wT[:, :], banks[3][0:E, :], ACT.Copy).then_inc(b_cwT.sem, 1)

            def exp_gate(i):
                act.wait_ge(b_lgs.sem, b_lgs.at(i, 1))
                av_(gw[1], gw[0], ACT.Exp).then_inc(b_ex.sem, 1)

            def layer1(i, p, first=False, last=False):
                copy_kv(i, 1, first)
                expert_step(i, p, 0, first)
                hidden_step(i, 1)
                copy_wT(i)
                weigh_expert(i, p, 0)
                exps(i, 0)
                start_y(i, p)
                copy_kv(i, 2, first)
                expert_step(i, p, 2)
                if not first:
                    tanh1(i - 1, 1 - p)
                    copy_oT(i - 1)
                if not last:
                    normalise1(i + 1)
                exps(i, 1)
                expert_step(i, p, 3)
                copy_kv(i, 3, first)
                if not last:
                    copy_xT(i + 1, 1 - p)
                expert_step(i, p, 4)
                exps(i, 2)
                if not first:
                    copy_sp(i - 1)
                expert_step(i, p, 5)
                if not last:
                    copy_kv(i + 1, 0, False)
                    exp_gate(i + 1)
                expert_step(i, p, 6)
                exps(i, 3)
                expert_step(i, p, 7, last=last)

            act.wait_ge(norm_ready, 1)
            normalise1(0, True)
            copy_xT(0, 0)
            exp_gate(0)
            copy_kv(0, 0, True)
            relu_hidden(0, 1, 0, edge=True)
            layer1(0, 0, first=True)
            with act.Fori(0, (NB - 2) // 2) as r:
                layer1(r * 2 + 1, 1)
                layer1(r * 2 + 2, 0)
            layer1(NB - 1, 1, last=True)
            weigh_expert(NB - 1, 1, E - 1)
            tanh1(NB - 1, 1)
            copy_oT(NB - 1)
            copy_sp(NB - 1)

        @block.vector
        def _(dve):
            own = Chain(dve, dve_own)
            link, add = own.link, own.add
            v = nc.vector
            dve.sem_inc(e_yv.sem, 2)
            v.memset(eps1[:, 0:1], EPS)
            v.memset(eps1[:, 1:2], 4 * EPS)
            link(v.memset(ones[:, :], 1.0))
            def stats(c):
                with dve.Fori(c * CH // 8, (c + 1) * CH // 8) as i:
                    for j in range(8):
                        t = bass.ds(i * 8 + j, 1)
                        v.bn_stats(st_all[:, t, :], x_all[:, t, :])

            def mean_var():
                me, qe, mo, qo = (st_all[:, :, n] for n in (1, 2, 4, 5))
                mean, var = mv_all[:, :, 0], mv_all[:, :, 1]
                link(v.tensor_tensor(mean, me, mo, ALU.subtract))
                link(v.scalar_tensor_tensor(var, mean, 0.25 * P, mean, ALU.mult, ALU.mult))
                link(v.tensor_tensor(var, var, qe, ALU.add))
                link(v.tensor_tensor(var, var, qo, ALU.add))
                link(v.tensor_scalar(var, var, 1.0 / P, None, ALU.mult))
                link(v.tensor_tensor(mean, me, mo, ALU.add))
                link(v.tensor_scalar(mean, mean, 0.5, None, ALU.mult))

            for c in range(NX):
                dve.wait_ge(x_in[c], 16)
                stats(c)
            dve.drain()
            mean_var()
            dve.sem_inc(var_ready, 1)
            dve.wait_ge(sd_ready, 1)
            link(v.reciprocal(rstd_all[:, :], rstd_all[:, :]))

            def weights0():
                dve.wait_ge(w_in, W_ALL)
                dve.wait_ge(w_decay, 1)
                v.tensor_scalar(decay[:, :], ones[:, :], ew[:, 1:2], None, ALU.mult)
                v.tensor_scalar(hbg[:, :], col(C_BG), 0.5, None, ALU.mult)
                link(v.tensor_scalar(omm[:, :], cols_sb[:, C_MIX:C_MIX + 4], -1.0, 1.0, ALU.mult, ALU.add))
                for n in range(4):
                    if n in MIXED:
                        continue
                    v.tensor_scalar(wm[:, n, 0, :], w4_sb[:, n, :], col(C_MIX + n), None, ALU.mult)
                    r = v.tensor_scalar(wm[:, n, 1, :], w4_sb[:, n, :], omm[:, n:n + 1], None, ALU.mult)
                r.then_inc(wm_ready, 1)

            def last_biases0():
                link(v.tensor_tensor(b2p[:, :, :], b2_bc[:, 0:E, :], b2_bc[:, 1:E + 1, :], ALU.add))
                link(v.tensor_scalar(b2p[:, :, :], b2p[:, :, :], 0.5, None, ALU.mult))

            def routing():
                wide = [P, NTILE, 2]
                link(v.tensor_tensor(x01, x_all[:, :, 0:2], mv_all[:, :, 0:1].to_broadcast(wide), ALU.subtract))
                link(v.tensor_tensor(x01, x01, rstd_all[:, :].unsqueeze(2).to_broadcast(wide), ALU.mult))
                c_sum, c_abs, c_fl, c_gt, c_sg, c_0 = cls[0:6]
                link(v.tensor_tensor(c_sum, x01[:, :, 0], x01[:, :, 1], ALU.add))
                link(v.tensor_scalar(c_sg, c_sum, 0.0, None, ALU.is_ge))
                link(v.tensor_scalar(c_sg, c_sg, 2.0, -1.0, ALU.mult, ALU.add))
                link(v.tensor_tensor(c_abs, c_sum, c_sg, ALU.mult))
                link(v.tensor_copy(clsi[0], c_abs))
                link(v.tensor_copy(c_fl, clsi[0]))
                link(v.tensor_tensor(c_gt, c_fl, c_abs, ALU.is_gt))
                link(v.tensor_tensor(c_fl, c_fl, c_gt, ALU.subtract))
                link(v.tensor_tensor(clsi[0], c_fl, c_sg, ALU.mult))
                link(v.tensor_scalar(clsi[1], clsi[0], 7, None, ALU.bitwise_and))
                link(v.tensor_copy(c_0, clsi[1]))
                full = [P, NTILE, E]
                v.tensor_tensor(oh3, iota.unsqueeze(1).to_broadcast(full), c_0.unsqueeze(2).to_broadcast(full), ALU.is_equal).then_inc(onehot_ready, 1)
                weights0()
                dve.wait_ge(counts_done, 1)
                before = banks[1][:, :].rearrange("p (n c) -> p n c", c=E)
                total = banks[2][:, :].rearrange("p (n c) -> p n c", c=E)
                for c in range(E):
                    last = v.tensor_tensor_scan(cum[:, c, :], ones[:, 0:NTILE], total[:, :, c], 0.0, ALU.mult, ALU.add)
                link(last)
                n_, nt, end, base = ncl
                link(v.tensor_scalar(ncli, cum[:, :, NTILE - 1], float(P - 1), None, ALU.add))
                link(v.tensor_scalar(ncli, ncli, P.bit_length() - 1, None, ALU.logical_shift_right))
                link(v.tensor_copy(nt, ncli))
                link(v.tensor_tensor_scan(end, ones[:, 0:E], nt, 0.0, ALU.mult, ALU.add))
                link(v.tensor_tensor(base, end, nt, ALU.subtract))
                link(v.tensor_scalar(base, base, float(P), None, ALU.mult))
                link(v.tensor_tensor(off, cum.rearrange("p c n -> p n c"), total, ALU.subtract))
                link(v.tensor_tensor(off, off, before, ALU.add))
                link(v.tensor_tensor(off, off, base.unsqueeze(1).to_broadcast(full), ALU.add))
                link(v.tensor_tensor(off, off, oh3, ALU.mult))
                link(v.tensor_reduce(posf, off, X, ALU.add))
                link(v.tensor_copy(pos_i[:, :], posf))
                every = [P, NTL, E]
                link(v.tensor_tensor(tcmp, end.unsqueeze(1).to_broadcast(every), tile_no.unsqueeze(2).to_broadcast(every), ALU.is_le))
                link(v.tensor_reduce(tcf, tcmp, X, ALU.add))
                link(v.tensor_scalar(tcls[:, :], tcf, float(E - 1), None, ALU.min))
                dve.sem_inc(route_ready, 1)

            routing()

            def rows0(n, p, before):
                if before is not None:
                    dve.wait_ge(a_scat[p], before * (16 * TB))
                    dve.wait_ge(a_xT.sem, a_xT.at(n - 1, 0))
                link(v.tensor_copy(idx[p], pos_i[:, tiles(n)]))
                v.tensor_copy(xnrow[p][:, :, P:RW].bitcast(i32), tid[:, tiles(n)].unsqueeze(2))
                for j in range(TB):
                    t = tile_of(n, j)
                    last = v.tensor_scalar(xnrow[p][:, j, 0:P], x_all[:, t, :], mv_all[:, t, 0], rstd_all[:, t], ALU.subtract, ALU.mult)
                last.then_inc(a_xn.sem, 1)

            def kv0(n):
                dve.wait_ge(a_v.sem, a_v.at(n, 1))
                dve.wait_ge(a_proj.sem, a_proj.at(n, 2))
                link(v.scalar_tensor_tensor(kv, banks[2][:, :], col(C_BK), v1, ALU.add, ALU.mult))

            def wkv0(n):
                for b in range(NSEQ):
                    s_ = slice(b * SEQ, (b + 1) * SEQ)
                    last = v.tensor_tensor_scan(acc[:, s_], decay[:, :], kv[:, s_], 0.0, ALU.mult, ALU.add)
                link(last)
                link(v.scalar_tensor_tensor(wkv, kv, col(C_U), acc, ALU.mult, ALU.add))
                dve.wait_ge(a_proj.sem, a_proj.at(n, 3))
                v.scalar_tensor_tensor(rw, banks[3][:, :], col(C_BR), wkv, ALU.add, ALU.mult).then_inc(a_rw.sem, 1)

            def mix0(n, p):
                dve.wait_ge(a_d.sem, a_d.at(n, 1))
                for m in MIXED:
                    last = v.scalar_tensor_tensor(byseq(mix[m][p]), byseq(diff), col(C_MIX + m), xnT[p][:, :, 0:SEQ], ALU.mult, ALU.add)
                last.then_inc(a_mix.sem, 1)

            def block0(i, p, before, first=False, left=3):
                dve.wait_ge(a_sq.sem, a_sq.at(i, 1))
                v.tensor_reduce(vs, sq.rearrange("p (h d) -> p h d", d=HD), X, ALU.add).then_inc(a_vs.sem, 1)
                if left >= 3:
                    rows0(i + 3, 1 - p, before)
                dve.wait_ge(a_sd.sem, a_sd.at(i, 1))
                link(v.reciprocal(rh, sd))
                v.tensor_tensor(o.rearrange("p (h d) -> p h d", d=HD), banks[5][:, :].rearrange("p (h d) -> p h d", d=HD),
                                rh.unsqueeze(2).to_broadcast([P, TB * H, HD]), ALU.mult).then_inc(a_o.sem, 1)
                if left >= 1:
                    kv0(i + 1)
                    wkv0(i + 1)
                dve.wait_ge(a_oTp.sem, a_oTp.at(i, 1))
                dve.wait_ge(a_th.sem, a_th.at(i, 1))
                v.scalar_tensor_tensor(oT, th[p], 1.0, banks[7][:, :], ALU.add, ALU.mult).then_inc(a_oT.sem, 1)
                if left >= 2:
                    dve.wait_ge(a_proj.sem, a_proj.at(i, 4))
                    mix0(i + 2, p)

            dve.wait_ge(tid_ready, 1)
            rows0(0, 0, None)
            rows0(1, 1, None)
            mix0(0, 0)
            rows0(2, 0, 1)
            kv0(0)
            wkv0(0)
            mix0(1, 1)
            block0(0, 0, 1, first=True)
            with dve.Fori(0, (NB - 4) // 2) as r:
                own.enter(r, 2 * 5)
                for p in (1, 0):
                    block0(r * 2 + (2 - p), p, r + 2)
            own.leave((NB - 4) // 2)
            for n in range(NB - 3, NB):
                block0(n, n % 2, None, left=NB - 1 - n)

            def class_weights(k, b):
                c = dve.value_load(tcls[0:1, bass.ds(k, 1)], min_val=0, max_val=E - 1)
                v.tensor_copy(wc[b], w1x[:, bass.ds(c, 2), :]).then_inc(e_wc.sem, 1)

            def outputs0(k, b):
                c = dve.value_load(tcls[0:1, bass.ds(k, 1)], min_val=0, max_val=E - 1)
                dve.wait_ge(e_y.sem, e_y.at(k, 1))
                v.scalar_tensor_tensor(ye[b].unsqueeze(1), banks[6 + b][:, 0:P].unsqueeze(1), 0.5, b2p[:, bass.ds(c, 1), :], ALU.mult, ALU.add).then_inc(e_yv.sem, 1)

            def silu0(k, u):
                b = u % 2
                dve.wait_ge(e_th.sem, e_th.at(k, 1))
                v.scalar_tensor_tensor(gout[u], the[b], 1.0, ye[b], ALU.add, ALU.mult).then_inc(e_g.sem, 1)

            def tile0(k, u, first=False, copy=True):
                b = u % 2
                dve.wait_ge(e_h.sem, e_h.at(k, 2))
                for c in range(FC):
                    r = v.tensor_scalar(hs[b][:, FC + c, :], banks[3 + 2 * b][:, c * P:(c + 1) * P], wc[b][:, 1, FF + c:FF + c + 1], 0.0, ALU.add, ALU.max)
                r.then_inc(e_r1.sem, 1)
                if not first:
                    outputs0(k - 1, 1 - b)
                if copy:
                    dve.wait_ge(e_r0.sem, e_r0.at(k, 1))
                    dve.wait_ge(e_r1.sem, e_r1.at(k, 1))
                    class_weights(k + 2, b)
                if not first:
                    silu0(k - 1, (u - 1) % NU)

            last_biases0()
            dve.wait_ge(we_in, WE_ALL)
            dve.wait_ge(a_se.sem, a_se.at(NB, 0))
            for p in range(2):
                dve.wait_ge(a_scat[p], NB // 2 * 16 * TB)
            class_weights(0, 0)
            class_weights(1, 1)
            for u in range(NU):
                tile0(u, u, first=(u == 0))
            with dve.Fori(1, NI - 1) as i:
                for u in range(NU):
                    tile0(i * NU + u, u)
            for u in range(NU):
                tile0(NTL - NU + u, u, copy=(u < NU - 2))
            outputs0(NTL - 1, 1)
            silu0(NTL - 1, NU - 1)

            dve.wait_ge(a_bo.sem, a_bo.at(NB, 0))
            for c in range(NX):
                c_ = slice(c * CH, (c + 1) * CH)
                dve.wait_ge(g_in[c], 16)
                v.scalar_tensor_tensor(s_all[:, c_, :], s_all[:, c_, :], 0.5, g_all[:, c_, :], ALU.mult, ALU.mult).then_inc(sg_ready, 1)
            for c in range(NX):
                dve.wait_ge(x1_ready, c + 1)
                stats(c)
            dve.drain()
            mean_var()
            dve.sem_inc(var2_ready, 1)
            dve.wait_ge(sd2_ready, 1)
            link(v.reciprocal(rstd_all[:, :], rstd_all[:, :]))
            v.tensor_scalar(hbp[:, :], bp_bc, 0.5, None, ALU.mult)
            v.scalar_tensor_tensor(nmr_all[:, :], mv_all[:, :, 0], -1.0, rstd_all[:, :], ALU.mult, ALU.mult).then_inc(norm_ready, 1)

            def scores(i, t):
                dve.wait_ge(b_kv.sem, b_kv.at(i, t + 1))
                q_b = banks[1 + t % 2][:, 0:3 * P].rearrange("p (h c) -> p h c", h=H)[:, :, 0:HD].unsqueeze(2).to_broadcast([P, H, H, HD])
                k_b = kvs[:, t, :, 0:HD].unsqueeze(1).to_broadcast([P, H, H, HD])
                v.tensor_tensor(prod.rearrange("p (h g d) -> p h g d", h=H, g=H), q_b, k_b, ALU.mult).then_inc(b_qk.sem, 1)
                dve.wait_ge(b_qk.sem, b_qk.at(i, t + 1))
                s3 = S[t % 2].rearrange("p (h g) -> p h g", h=H)
                link(v.tensor_reduce(S[t % 2], prod.rearrange("p (s d) -> p s d", d=HD), X, ALU.add))
                link(v.tensor_reduce(mx[t % 2], s3, X, ALU.max))
                v.tensor_tensor(s3, s3, mx[t % 2].unsqueeze(2).to_broadcast([P, H, H]), ALU.subtract).then_inc(b_sc.sem, 1)

            def denominators(i, t):
                dve.wait_ge(b_a.sem, b_a.at(i, t + 1))
                t_ = slice(t * H, (t + 1) * H)
                link(v.tensor_reduce(den[:, t_], A[t % 2].rearrange("p (h g) -> p h g", h=H), X, ALU.add))
                link(v.reciprocal(rden[:, t_], den[:, t_]))

            def heads_out(i, t):
                s_, n = av_summed(t)
                if t in PE_AV:
                    dve.wait_ge(s_.sem, s_.at(i, n))
                    src = banks[7][:, t * P:(t + 1) * P]
                else:
                    dve.wait_ge(b_av.sem, b_av.at(i, t + 1))
                    v.tensor_reduce(red, av[t % 2].rearrange("p (g o) -> p o g", g=H), X, ALU.add).then_inc(b_avr.sem, 1)
                    dve.wait_ge(s_.sem, s_.at(i, n))
                    src = red
                v.tensor_tensor(o1[:, t * P:(t + 1) * P].rearrange("p (h d) -> p h d", d=HD), src.rearrange("p (h d) -> p h d", d=HD),
                                rden[:, t * H:(t + 1) * H].unsqueeze(2).to_broadcast([P, H, HD]), ALU.mult).then_inc(b_of.sem, 1)

            lg, ex, pr, oh, sc = gw
            m_, r_, z_, z2 = sm
            rv = rev.unsqueeze(1).to_broadcast([P, TB, E])

            def b_(a):
                return a.unsqueeze(2).to_broadcast([P, TB, E])

            def logits(i):
                dve.wait_ge(b_lg.sem, b_lg.at(i, 1))
                link(v.tensor_tensor(lg, banks[0][:, 0:TB * E].rearrange("p (j e) -> p j e", j=TB),
                                     gateb_bc.unsqueeze(1).to_broadcast([P, TB, E]), ALU.add))
                link(v.tensor_reduce(m_, lg, X, ALU.max))
                v.tensor_tensor(lg, lg, b_(m_), ALU.subtract).then_inc(b_lgs.sem, 1)

            def routed(i, p, first=False):
                dve.wait_ge(b_ex.sem, b_ex.at(i, 1))
                link(v.tensor_reduce(z_, ex, X, ALU.add))
                link(v.reciprocal(z2, z_))
                link(v.tensor_tensor(pr, ex, b_(z2), ALU.mult))
                link(v.tensor_reduce(m_, pr, X, ALU.max))
                link(v.tensor_tensor(oh, pr, b_(m_), ALU.is_equal))
                link(v.tensor_tensor(sc, oh, rv, ALU.mult))
                link(v.tensor_reduce(r_, sc, X, ALU.max))
                link(v.tensor_tensor(oh, rv, b_(r_), ALU.is_equal))
                link(v.scalar_tensor_tensor(ex, oh, -2.0, pr, ALU.mult, ALU.add))
                link(v.tensor_reduce(m_, ex, X, ALU.max))
                link(v.tensor_tensor(lg, ex, b_(m_), ALU.is_equal))
                link(v.tensor_tensor(sc, lg, rv, ALU.mult))
                link(v.tensor_reduce(r_, sc, X, ALU.max))
                link(v.tensor_tensor(lg, rv, b_(r_), ALU.is_equal))
                if not first:
                    dve.wait_ge(b_ys.sem, b_ys.at(i, -E))
                link(v.tensor_tensor(oh, oh, b_(pr[:, :, 0]), ALU.mult))
                link(v.tensor_tensor(lg, lg, b_(pr[:, :, 1]), ALU.mult))
                v.tensor_tensor(cw_[p], oh, lg, ALU.add).then_inc(b_cw.sem, 1)

            def gated(i, p):
                dve.wait_ge(b_th.sem, b_th.at(i, 1))
                dve.wait_ge(b_fin.sem, b_fin.at(i, 0))
                v.scalar_tensor_tensor(gy, th1, 1.0, y[p], ALU.add, ALU.mult).then_inc(b_gy.sem, 1)

            def layer1(i, p, first=False, last=False):
                if not first:
                    heads_out(i - 1, 2)
                scores(i, 0)
                if not first:
                    denominators(i - 1, 3)
                    heads_out(i - 1, 3)
                scores(i, 1)
                denominators(i, 0)
                if not first:
                    gated(i - 1, 1 - p)
                    dve.wait_ge(b_oTp.sem, b_oTp.at(i - 1, 1))
                heads_out(i, 0)
                scores(i, 2)
                denominators(i, 1)
                if not last:
                    logits(i + 1)
                heads_out(i, 1)
                scores(i, 3)
                denominators(i, 2)
                if not last:
                    routed(i + 1, 1 - p, first)

            logits(0)
            routed(0, 0, True)
            layer1(0, 0, first=True)
            with dve.Fori(0, (NB - 2) // 2) as r:
                own.enter(r, 2 * (16 + 2 + 4 * TB))
                layer1(r * 2 + 1, 1)
                layer1(r * 2 + 2, 0)
            own.leave((NB - 2) // 2)
            layer1(NB - 1, 1, last=True)
            heads_out(NB - 1, 2)
            denominators(NB - 1, 3)
            heads_out(NB - 1, 3)
            gated(NB - 1, 1)

        @block.tensor
        def _(pe):
            mm = nc.tensor.matmul

            def tr(src, done, dst=0):
                for j in range(TB):
                    last = nc.tensor.transpose(banks[dst][:, j * P:(j + 1) * P], src[:, j, :], ident[:, :])
                last.then_inc(done.sem, 1)

            def token_major(dst, src, rhs, done):
                for j in range(TB):
                    last = mm(dst[:, j * P:(j + 1) * P], src[:, j * P:(j + 1) * P], rhs, start=True, stop=True)
                last.then_inc(done.sem, 1)

            pe.wait_ge(w_in, W_ALL)
            pe.wait_ge(onehot_ready, 1)
            mm(banks[1][:, :], below[:, :], onehot, start=True, stop=True)
            mm(banks[2][:, :], ones[:, 0:P], onehot, start=True, stop=True).then_inc(counts_done, 1)

            def rows_T0(n, p):
                pe.wait_ge(a_xn.sem, a_xn.at(n, 1))
                tr(xnrow[p][:, :, 0:P], a_xT)

            def project0(n, p, first=False):
                pe.wait_ge(a_xnT.sem, a_xnT.at(n, 1))
                for m, b in ((V_, 1), (K_, 2), (R_, 3), (G_, 4)):
                    dst = banks[b][:, :].rearrange("p (b t) -> p b t", b=NSEQ)
                    if m == G_ and not first:
                        pe.wait_ge(a_th.sem, a_th.at(n, 0))
                    if m in MIXED:
                        pe.wait_ge(a_mix.sem, a_mix.at(n, 1))
                        mm(dst, w4_sb[:, m, :], byseq(mix[m][p]), start=True, stop=True).then_inc(a_proj.sem, 1)
                    else:
                        mm(dst, wm[:, m, 0, :], xnT[p][:, :, 1:SEQ + 1], start=True, stop=False)
                        mm(dst, wm[:, m, 1, :], xnT[p][:, :, 0:SEQ], start=False, stop=True).then_inc(a_proj.sem, 1)

            def out_w0(n):
                pe.wait_ge(a_oT.sem, a_oT.at(n, 1))
                pe.wait_ge(a_se.sem, a_se.at(n, 0))
                token_major(banks[6], oT, wo_sb[:, :], a_s)

            def block0(i, p, first=False, left=3):
                if left >= 2:
                    pe.wait_ge(a_xnT.sem, a_xnT.at(i + 1, 1))
                    rows_T0(i + 2, p)
                pe.wait_ge(a_rw.sem, a_rw.at(i, 1))
                token_major(banks[5], rw, center[:, :], a_c)
                if not first:
                    out_w0(i - 1)
                if left >= 1:
                    project0(i + 1, 1 - p)
                pe.wait_ge(a_o.sem, a_o.at(i, 1))
                tr(byt(o), a_oTp, 7)

            pe.wait_ge(wm_ready, 1)
            pe.wait_ge(route_ready, 1)
            rows_T0(0, 0)
            pe.wait_ge(a_xnT.sem, a_xnT.at(0, 1))
            rows_T0(1, 1)
            project0(0, 0, first=True)
            block0(0, 0, first=True)
            with pe.Fori(0, (NB - 4) // 2) as r:
                for p in (1, 0):
                    block0(r * 2 + (2 - p), p)
            for n in range(NB - 3, NB):
                block0(n, n % 2, left=NB - 1 - n)
            out_w0(NB - 1)

            def rows_T1(k, ku, loads):
                pe.wait_ge(e_ld[ku], loads * 16)
                b = ku % 2
                nc.tensor.transpose(banks[0][:, b * P:(b + 1) * P], xsb[ku][:, 0:P], ident[:, :]).then_inc(e_T.sem, 1)

            def hidden0(k, ku):
                b = ku % 2
                pe.wait_ge(e_xs.sem, e_xs.at(k, 1))
                pe.wait_ge(e_wc.sem, e_wc.at(k, 1))
                for e in range(2):
                    for c in range(FC):
                        last = mm(banks[2 + 2 * b + e][:, c * P:(c + 1) * P], wc[b][:, e, c * P:(c + 1) * P], xsT[b], start=True, stop=True)
                    last.then_inc(e_h.sem, 1)

            def out0(k, u):
                b = u % 2
                cl = pe.value_load(tcls[0:1, bass.ds(k, 1)], min_val=0, max_val=E - 1)
                pe.wait_ge(e_yv.sem, e_yv.at(k, -1))
                for e in range(2):
                    pe.wait_ge((e_r0, e_r1)[e].sem, (e_r0, e_r1)[e].at(k, 1))
                    for c in range(FC):
                        n = e * FC + c
                        last = mm(banks[6 + b][:, 0:P], hs[b][:, n, :], w2x[:, bass.ds(cl + e, 1), c, :],
                                  start=(n == 0), stop=(n == 2 * FC - 1))
                last.then_inc(e_y.sem, 1)

            pe.wait_ge(we_in, WE_ALL)
            def tile0(k, u, loads, left=2):
                if left >= 1:
                    hidden0(k + 1, (u + 1) % NU)
                if left >= 2:
                    rows_T1(k + 2, (u + 2) % NU, loads + (u + 2) // NU)
                out0(k, u)

            rows_T1(0, 0, 1)
            pe.wait_ge(e_xs.sem, e_xs.at(0, 1))
            rows_T1(1, 1, 1)
            hidden0(0, 0)
            for u in range(NU):
                tile0(u, u, 1)
            with pe.Fori(1, NI - 1) as i:
                for u in range(NU):
                    tile0(i * NU + u, u, i + 1)
            for u in range(NU):
                tile0(NTL - NU + u, u, NI, NU - 1 - u)

            def hidden1(i, p, n, e, edge=False):
                k = hid(n, e, edge)
                pe.wait_ge(b_hs.sem, b_hs.at(i, k - 2))
                mm(banks[4 + k % 2][:, :], l_sb[n - 1][:, e, :], xT[p] if n == 1 else h1s[e % 2], start=True, stop=True).then_inc(b_h.sem, 1)

            def out1(i, e, last=False):
                pe.wait_ge(b_hs.sem, b_hs.at(i, hid(2, e, last)))
                pe.wait_ge(b_ys.sem, b_ys.at(i, e))
                token_major(banks[6], h2s[e % 2], l_sb[2][:, e, :], b_y)

            def hidden_step(i, p, e, last=False):
                if e < E - 1:
                    hidden1(i, p, 1, e + 1)
                elif not last:
                    hidden1(i + 1, 1 - p, 1, 0)
                hidden1(i, p, 2, e, last)

            def expert_step(i, p, e, first=False, last=False):
                hidden_step(i, p, e, last)
                if e:
                    out1(i, e - 1)
                elif not first:
                    out1(i - 1, E - 1)

            def qkv1(i, p, t, first=False):
                if not first:
                    pe.wait_ge(b_qk.sem, b_qk.at(i, t - 1))
                mm(banks[1 + t % 2][:, 0:3 * P], xT[p][:, t * P:(t + 1) * P], wqkv_sb[:, :], start=True, stop=True).then_inc(b_qkvp.sem, 1)

            def gate1(i, p):
                pe.wait_ge(b_xq.sem, b_xq.at(i, 1))
                for j in range(TB):
                    last = mm(banks[0][:, j * E:(j + 1) * E], xT[p][:, j * P:(j + 1) * P], gate_sb[:, :], start=True, stop=True)
                last.then_inc(b_lg.sem, 1)

            def next_T(i):
                pe.wait_ge(b_xn.sem, b_xn.at(i, 1))
                tr(xn1, b_xT)

            def sum_heads(i, t, first=False):
                if t not in PE_AV:
                    return
                pe.wait_ge(b_av.sem, b_av.at(i, t + 1))
                if not (first and t == 0):
                    pe.wait_ge(b_of.sem, b_of.at(i, t))
                for g in range(H):
                    last = mm(banks[7][:, t * P:(t + 1) * P], ident[:, :], av[t % 2][:, g * P:(g + 1) * P], start=(g == 0), stop=(g == H - 1))
                last.then_inc(b_avp.sem, 1)

            def heads_T(i):
                pe.wait_ge(b_of.sem, b_of.at(i + 1, 0))
                tr(byt(o1), b_oTp)

            def project(i):
                pe.wait_ge(b_oT.sem, b_oT.at(i, 1))
                token_major(banks[3], oT1, wproj_sb[:, :], b_s)

            def weights_T(i, p):
                pe.wait_ge(b_cw.sem, b_cw.at(i, 1))
                for j in range(TB):
                    r = nc.tensor.transpose(banks[3][0:E, j * P:(j + 1) * P], cw_[p][:, j, :], ident[:, :])
                r.then_inc(b_cwTp.sem, 1)

            def biases(i):
                pe.wait_ge(b_cwT.sem, b_cwT.at(i, 1))
                token_major(banks[3], wT, b3_sb[:, :], b_y0)

            def layer1(i, p, first=False, last=False):
                qkv1(i, p, 1, first)
                expert_step(i, p, 0, first)
                if not first:
                    sum_heads(i - 1, 3)
                hidden_step(i, p, 1)
                weights_T(i, p)
                out1(i, 0)
                qkv1(i, p, 2)
                biases(i)
                expert_step(i, p, 2)
                if not first:
                    heads_T(i - 1)
                sum_heads(i, 0, first)
                expert_step(i, p, 3)
                qkv1(i, p, 3)
                if not last:
                    if not first:
                        pe.wait_ge(b_oT.sem, b_oT.at(i - 1, 1))
                    next_T(i + 1)
                expert_step(i, p, 4)
                if not last:
                    gate1(i + 1, 1 - p)
                sum_heads(i, 1)
                if not first:
                    project(i - 1)
                expert_step(i, p, 5)
                if not last:
                    qkv1(i + 1, 1 - p, 0)
                expert_step(i, p, 6)
                sum_heads(i, 2)
                expert_step(i, p, 7, last=last)

            pe.wait_ge(wb_in, WB_ALL)
            next_T(0)
            gate1(0, 0)
            qkv1(0, 0, 0, True)
            hidden1(0, 0, 1, 0, edge=True)
            layer1(0, 0, first=True)
            with pe.Fori(0, (NB - 2) // 2) as r:
                layer1(r * 2 + 1, 1)
                layer1(r * 2 + 2, 0)
            layer1(NB - 1, 1, last=True)
            out1(NB - 1, E - 1, last=True)
            sum_heads(NB - 1, 3)
            heads_T(NB - 1)
            project(NB - 1)


def kernel(**inputs):
    import numpy as _np
    import concourse.bacc as _bacc
    from concourse import mybir as _mybir
    from concourse.bass_utils import run_bass_kernel_spmd as _run

    a = {k: _np.asarray(v) for k, v in inputs.items()}
    x = a["L0_attn_x"]
    c = _np.ascontiguousarray
    names = ["mg", "mr", "mk", "mv", "Wr_b", "Wk_b", "Wv_b"]
    cols = [a["L0_attn_" + n].reshape(P) for n in names] + [a["L0_attn_u"].reshape(P), a["L0_attn_w"].reshape(P)]
    cols += list(a["L1_ffn_b1"]) + list(a["L1_ffn_b2"]) + [a["L0_attn_Wg_b"]]
    idx = _np.arange(P)
    same_head = (idx[:, None] // HD == idx[None, :] // HD).astype(_np.float32)
    eye = _np.eye(P, dtype=_np.float32)
    below = (idx[:, None] < idx[None, :]).astype(_np.float32)
    steps = _np.arange(E, dtype=_np.float32)
    ntl = -(-(x.shape[0] * x.shape[1] // P + E - 1) // NU) * NU
    w1b = _np.concatenate([a["L0_ffn_W1"], a["L0_ffn_b1"].reshape(E, FC, P).transpose(0, 2, 1)], axis=2)
    arrays = {
        "x": c(x.reshape(-1, P)),
        "w4": c(_np.stack([a[f"L0_attn_W{n}_w"].T for n in "grkv"], axis=1)),
        "wo": c(a["L0_attn_Wo_w"].T),
        "w1b": c(_np.concatenate([w1b, w1b[:1]])),
        "w2": c(a["L0_ffn_W2"]),
        "wqkv": c(a["L1_attn_Wqkv"].T),
        "wproj": c(a["L1_attn_Wproj"].T),
        "gate": c(a["L1_ffn_gate_w"].T),
        "l1": c(a["L1_ffn_w1"]), "l2": c(a["L1_ffn_w2"]), "l3": c(a["L1_ffn_w3"]),
        "cols": c(_np.stack(cols, axis=1)),
        "rows": c(_np.concatenate([a["L0_attn_Wo_b"], a["L1_attn_bproj"], a["L1_ffn_gate_b"], steps, E - steps,
                                   _np.arange(ntl, dtype=_np.float32)])),
        "b2": c(_np.concatenate([a["L0_ffn_b2"], a["L0_ffn_b2"][:1]])), "b3": c(a["L1_ffn_b3"]),
        "consts": _np.stack([eye, eye - same_head / HD, below]).astype(_np.float32),
    }
    nc = _bacc.Bacc("TRN2", target_bir_lowering=False, num_devices=1)
    args = [nc.dram_tensor("in_" + n, v.shape, _mybir.dt.from_np(v.dtype), kind="ExternalInput").ap() for n, v in arrays.items()]
    out = nc.dram_tensor("out_0", arrays["x"].shape, _mybir.dt.float32, kind="ExternalOutput").ap()
    two_layers(nc, *args, out)
    r = _run(nc, [{"in_" + n: v for n, v in arrays.items()}], core_ids=[0])
    return r.results[0]["out_0"].reshape(x.shape)
```

```python
import concourse.bass as bass
from concourse import mybir
from contextlib import ExitStack

P = 128
TB = 4
NT = TB * P
SEQ = 256
NSEQ = NT // SEQ
H, HD = 16, 8
E = 8
FF = 512
FC = FF // P
EPS = 1e-5
C_MIX = 0
C_BR, C_BK, C_BV, C_U, C_W = 4, 5, 6, 7, 8
C_LB1 = 9
C_LB2 = C_LB1 + E
C_BG = C_LB2 + E
NCOL = C_BG + 1
PE_AV = (2,)
POOL_MAX = (0,)
G_, R_, K_, V_ = 0, 1, 2, 3
MIXED = (R_, G_)
RW = P + 1
NU = 6


class Signal:

    def __init__(self, sem, per, start=0):
        self.sem, self.per, self.start = sem, per, start

    def at(self, i, n):
        return i * self.per + (n + self.start)


class Chain:

    def __init__(self, eng, sem):
        self.eng, self.sem, self.base, self.n, self.i, self.per, self.first = eng, sem, 0, 0, 0, 0, 0

    def enter(self, i, per, start=0):
        self.base += self.n
        self.first = start * per
        self.i, self.per, self.n = i, per, 0

    def leave(self, blocks):
        assert self.n == self.per, f"chain: {self.n} steps, not {self.per}"
        self.base += blocks * self.per
        self.i, self.per, self.n, self.first = 0, 0, 0, 0

    def add(self, ins):
        ins.then_inc(self.sem, 1)
        self.n += 1
        return self.i * self.per + (self.base + self.n - self.first)

    def link(self, ins):
        self.eng.wait_ge(self.sem, self.add(ins))


def two_layers(nc, x, w4, wo, w1b, w2, wqkv, wproj, gate, l1, l2, l3, cols, rows, b2, b3, consts, out):
    fp = mybir.dt.float32
    i32 = mybir.dt.int32
    ALU = mybir.AluOpType
    ACT = mybir.ActivationFunctionType
    X = mybir.AxisListType.X

    ntok = x.shape[0]
    NTILE = ntok // P
    NB = ntok // NT
    NTL = -(-(NTILE + E - 1) // NU) * NU
    NONE = 1 << 24
    WB = FF + FC

    xs = nc.dram_tensor("xs", [NTL * P, RW], fp).ap()
    gs = nc.dram_tensor("gs", [ntok, P], fp).ap()

    ctx = ExitStack()
    with ctx:
        def sb(name, shape, dt=fp):
            return ctx.enter_context(nc.sbuf_tensor(name, shape, dt))

        def bank(name):
            return ctx.enter_context(nc.psum_tensor(name, [P, 512], fp))

        def sem(name):
            return ctx.enter_context(nc.semaphore(name))

        def signal(name, per=1, start=0):
            return Signal(sem(name), per, start)

        x_all = sb("x_all", [P, NTILE, P])
        s_all = sb("s_all", [P, NTILE, P])
        st_all = sb("st_all", [P, NTILE, 6])
        mv_all = sb("mv_all", [P, NTILE, 2])
        rstd_all = sb("rstd_all", [P, NTILE])
        pos_i = sb("pos_i", [P, NTILE], i32)
        tid = sb("tid", [P, NTILE], i32)
        tcls = sb("tcls", [P, NTL], i32)
        w4_sb = sb("w4_sb", [P, 4, P])
        wm = sb("wm", [P, 4, 2, P])
        wo_sb = sb("wo_sb", [P, P])
        wqkv_sb = sb("wqkv_sb", [P, 3 * P])
        wproj_sb = sb("wproj_sb", [P, P])
        gate_sb = sb("gate_sb", [P, E])
        wts = sb("wts", [P, (E + 1) * WB + (E + 1) * FF])
        w1x = wts[:, 0:(E + 1) * WB].rearrange("p (e f) -> p e f", e=E + 1)
        w2x = wts[:, (E + 1) * WB:(E + 1) * (WB + FF)].rearrange("p (e c d) -> p e c d", e=E + 1, c=FC)
        g_all = wts[:, 0:ntok].rearrange("p (n d) -> p n d", d=P)
        l_sb = [sb(f"l{n}_sb", [P, E, P]) for n in (1, 2, 3)]
        cols_sb = sb("cols_sb", [P, NCOL])
        omm = sb("omm", [P, 4])
        hbg = sb("hbg", [P, 1])
        rows_sb = sb("rows_sb", [P, 2 * P + 3 * E + NTL])
        bo_bc, bp_bc = (rows_sb[:, n * P:(n + 1) * P] for n in range(2))
        gateb_bc = rows_sb[:, 2 * P:2 * P + E]
        iota = rows_sb[:, 2 * P + E:2 * P + 2 * E]
        rev = rows_sb[:, 2 * P + 2 * E:2 * P + 3 * E]
        tile_no = rows_sb[:, 2 * P + 3 * E:2 * P + 3 * E + NTL]
        b2_bc = sb("b2_bc", [P, E + 1, P])
        b2p = sb("b2p", [P, E, P])
        b3_sb = sb("b3_sb", [E, P])
        ident = sb("ident", [P, P])
        center = sb("center", [P, P])
        below = sb("below", [P, P])
        decay = sb("decay", [P, SEQ])
        ew = sb("ew", [P, 2])
        ones = sb("ones", [P, SEQ])
        eps1 = sb("eps1", [P, 2])

        WORK = 16384
        work = sb("work", [P, WORK])
        used = [0]

        def part(n):
            used[0] += n
            assert used[0] <= WORK
            return work[:, used[0] - n:used[0]]

        def lay(ap, pat, **kw):
            return ap.rearrange(pat, **kw)

        banks = [bank(f"bank{n}") for n in range(8)]

        used[0] = 9 * NT + 3 * TB * H
        fill = lay(part(9 * RW), "p (a r) -> p a r", r=RW)
        xnrow = [lay(part(TB * RW), "p (j r) -> p j r", j=TB) for _ in range(4)]
        idx = [part(TB).bitcast(i32) for _ in range(2)]
        xnT = [lay(part(NSEQ * (SEQ + 1)), "p (b t) -> p b t", b=NSEQ) for _ in range(2)]
        th = [part(NT) for _ in range(2)]
        mix = {m: [part(NT) for _ in range(2)] for m in MIXED}
        diff = part(NT)
        cls = [part(NTILE) for _ in range(8)]
        clsi = [part(NTILE).bitcast(i32) for _ in range(2)]
        x01 = lay(part(2 * NTILE), "p (n a) -> p n a", a=2)
        onehot = part(NTILE * E)
        oh3 = lay(onehot, "p (n c) -> p n c", c=E)
        cum = lay(part(NTILE * E), "p (c n) -> p c n", c=E)
        off = lay(part(NTILE * E), "p (n c) -> p n c", c=E)
        ncl = [part(E) for _ in range(4)]
        ncli = part(E).bitcast(i32)
        tcmp = lay(part(NTL * E), "p (k c) -> p k c", c=E)
        tcf = part(NTL)
        posf = part(NTILE)
        used[0] = 0
        v1, kv, acc, wkv, rw, sq, o, oT = (part(NT) for _ in range(8))
        vs, sd, rh = (part(TB * H) for _ in range(3))
        used[0] = 0
        xsb = [part(RW) for _ in range(NU)]
        gout = [part(P) for _ in range(NU)]
        xsT = [part(P) for _ in range(2)]
        wc = [lay(part(2 * WB), "p (e f) -> p e f", e=2) for _ in range(2)]
        hs = [lay(part(2 * FF), "p (n t) -> p n t", t=P) for _ in range(2)]
        ye = [part(P) for _ in range(2)]
        the = [part(P) for _ in range(2)]
        used[0] = 0
        xn1 = lay(part(NT), "p (j d) -> p j d", j=TB)
        xT = [part(NT) for _ in range(2)]
        kvs = lay(part(TB * 2 * P), "p (j h c) -> p j h c", j=TB, h=H)
        prod = part(H * H * HD)
        av = [part(H * H * HD) for _ in range(2)]
        S = [part(H * H) for _ in range(2)]
        A = [part(H * H) for _ in range(2)]
        mx = [part(H) for _ in range(2)]
        den, rden = part(TB * H), part(TB * H)
        red = part(P)
        o1, oT1, th1, gy = (part(NT) for _ in range(4))
        y = [part(NT) for _ in range(2)]
        ysc = [part(NT) for _ in range(2)]
        h1s = [part(NT) for _ in range(2)]
        gw = [lay(part(TB * E), "p (j e) -> p j e", j=TB) for _ in range(6)]
        p01 = lay(part(TB * 2), "p (j e) -> p j e", j=TB)
        cw_ = [lay(part(TB * E), "p (j e) -> p j e", j=TB) for _ in range(2)]
        sm = [part(TB) for _ in range(4)]
        nmr_all, hbp = part(NTILE), part(P)
        h2s = [wts[:, n * NT:(n + 1) * NT] for n in range(2)]
        obuf = lay(wts[:, 2 * NT:3 * NT], "p (j d) -> p j d", j=TB)
        wT = wts[0:E, 3 * NT:4 * NT]
        fin, sp1 = (wts[:, n * NT:(n + 1) * NT] for n in (4, 5))

        NX = 8
        CH = NTILE // NX

        x_in = [sem(f"x_in{c}") for c in range(NX)]
        w_in = sem("w_in")
        we_in = sem("we_in")
        wb_in = sem("wb_in")
        g_in = [sem(f"g_in{c}") for c in range(NX)]
        fill_ready, fill_done = sem("fill_ready"), sem("fill_done")
        tid_ready = sem("tid_ready")
        out_done = sem("out_done")
        dve_own, act_own = sem("dve_own"), sem("act_own")
        pool_turn = sem("pool_turn")
        w_decay = sem("w_decay")
        wm_ready = sem("wm_ready")
        var_ready, sd_ready = sem("var_ready"), sem("sd_ready")
        var2_ready, sd2_ready = sem("var2_ready"), sem("sd2_ready")
        norm_ready = sem("norm_ready")
        onehot_ready, counts_done = sem("onehot_ready"), sem("counts_done")
        route_ready = sem("route_ready")
        sg_ready, x1_ready = sem("sg_ready"), sem("x1_ready")
        a_xn = signal("a_xn")
        a_scat = [sem(f"a_scat{p}") for p in range(2)]
        a_xT = signal("a_xT")
        a_xnT = signal("a_xnT")
        a_d = signal("a_d")
        a_mix = signal("a_mix")
        a_proj = signal("a_proj", 4)
        a_v = signal("a_v")
        a_rw = signal("a_rw")
        a_th = signal("a_th")
        a_c = signal("a_c")
        a_sq = signal("a_sq")
        a_vs = signal("a_vs")
        a_sd = signal("a_sd")
        a_o = signal("a_o")
        a_oTp = signal("a_oTp")
        a_oT = signal("a_oT")
        a_s = signal("a_s")
        a_se = signal("a_se", 1, 1)
        a_bo = signal("a_bo")
        e_ld = [sem(f"e_ld{u}") for u in range(NU)]
        e_sc = [sem(f"e_sc{u}") for u in range(NU)]
        e_wc = signal("e_wc")
        e_T = signal("e_T")
        e_xs = signal("e_xs")
        e_h = signal("e_h", 2)
        e_r0 = signal("e_r0")
        e_r1 = signal("e_r1")
        e_y = signal("e_y")
        e_yv = signal("e_yv", 1, 2)
        e_th = signal("e_th")
        e_g = signal("e_g")
        b_xn = signal("b_xn")
        b_xT = signal("b_xT")
        b_xq = signal("b_xq")
        b_lg = signal("b_lg")
        b_lgs = signal("b_lgs")
        b_ex = signal("b_ex")
        b_cw = signal("b_cw")
        b_cwTp = signal("b_cwTp")
        b_cwT = signal("b_cwT")
        b_y0 = signal("b_y0")
        b_yi = signal("b_yi")
        b_qkvp = signal("b_qkvp", TB)
        b_kv = signal("b_kv", TB)
        b_qk = signal("b_qk", TB)
        b_mx = signal("b_mx", max(1, len(POOL_MAX)))
        b_sc = signal("b_sc", TB)
        b_a = signal("b_a", TB)
        b_av = signal("b_av", TB)
        b_avp = signal("b_avp", max(1, len(PE_AV)))
        b_avr = signal("b_avr", max(1, TB - len(PE_AV)))
        b_of = signal("b_of", TB)
        b_oTp = signal("b_oTp")
        b_oT = signal("b_oT")
        b_s = signal("b_s")
        b_h = signal("b_h", 2 * E)
        b_hs = signal("b_hs", 2 * E, 2)
        b_y = signal("b_y", E)
        b_ys = signal("b_ys", E, 1)
        b_ya = signal("b_ya", E, 2)
        b_tt = signal("b_tt")
        b_th = signal("b_th")
        b_gy = signal("b_gy", 1, 1)
        b_sp = signal("b_sp")
        b_sb = signal("b_sb")
        b_fin = signal("b_fin", 1, 1)
        b_out = signal("b_out")

        def hid(n, e, edge=False):
            if n == 1:
                return 1 if edge else 2 * e
            return 2 * e + 3 - edge

        def tiles(i):
            return bass.ds(i * TB, TB)

        def tile_of(i, j):
            return bass.ds(i * TB + j, 1)

        def col(n):
            return cols_sb[:, n:n + 1]

        def byt(ap):
            return ap.rearrange("p (j d) -> p j d", j=TB)

        def byseq(ap):
            return ap.rearrange("p (b t) -> p b t", b=NSEQ)

        def av_summed(t):
            pe = [u for u in range(TB) if u in PE_AV]
            no = [u for u in range(TB) if u not in PE_AV]
            return (b_avp, pe.index(t) + 1) if t in pe else (b_avr, no.index(t) + 1)

        block = ctx.enter_context(nc.Block())

        x_v = x.rearrange("(n p) d -> p n d", p=P)
        g_v = gs.rearrange("(n p) d -> p n d", p=P)
        xs_v = xs.rearrange("(k p) r -> k p r", p=P)
        NI = NTL // NU
        W_ALL, WB_ALL, WE_ALL = 16 * 8, 16 * 7, 16 * 3

        @block.sync
        def _(sp):
            for c in range(NX):
                sp.dma_start(x_all[:, c * CH:(c + 1) * CH, :], x_v[:, c * CH:(c + 1) * CH, :]).then_inc(x_in[c], 16)
            sp.dma_start(rows_sb[:, :], rows.partition_broadcast(P)).then_inc(w_in, 16)
            sp.dma_start(cols_sb[:, :], cols).then_inc(w_in, 16)
            for n, m in enumerate((ident, center, below)):
                sp.dma_start(m[:, :], consts[n]).then_inc(w_in, 16)
            sp.dma_start(w4_sb[:, :, :], w4).then_inc(w_in, 16)
            sp.dma_start(wo_sb[:, :], wo).then_inc(w_in, 16)
            sp.dma_start(b2_bc[:, :, :], b2.rearrange("e d -> (e d)").partition_broadcast(P).rearrange("p (e d) -> p e d", e=E + 1)).then_inc(w_in, 16)
            sp.wait_ge(fill_ready, 1)
            for n in range(NTL // 9):
                sp.dma_start(xs_v[n * 9:(n + 1) * 9].rearrange("k p r -> p k r"), fill).then_inc(fill_done, 16)
            sp.dma_start(w1x, w1b.rearrange("e d f -> d e f")).then_inc(we_in, 16)
            sp.dma_start(w2x[:, 0:E], w2.rearrange("e (c p) d -> p e c d", p=P)).then_inc(we_in, 16)
            sp.dma_start(w2x[:, E], w2[0].rearrange("(c p) d -> p c d", p=P)).then_inc(we_in, 16)
            sp.dma_start(b3_sb[:, :], b3).then_inc(wb_in, 16)
            sp.dma_start(wqkv_sb[:, :], wqkv).then_inc(wb_in, 16)
            sp.dma_start(wproj_sb[:, :], wproj).then_inc(wb_in, 16)
            sp.dma_start(gate_sb[:, :], gate).then_inc(wb_in, 16)
            for n, lw in enumerate((l1, l2, l3)):
                sp.dma_start(l_sb[n][:, :, :], lw.rearrange("e d f -> d e f")).then_inc(wb_in, 16)

            for p in range(2):
                sp.wait_ge(a_scat[p], NB // 2 * 16 * TB)
            sp.wait_ge(a_se.sem, a_se.at(NB, 0))
            for u in range(NU):
                sp.dma_start(xsb[u], xs_v[u]).then_inc(e_ld[u], 16)
            with sp.Fori(1, NI) as i:
                for u in range(NU):
                    sp.wait_ge(e_sc[u], i * 16)
                    sp.dma_start(xsb[u], xs_v[bass.ds(i * NU + u, 1)].rearrange("k p r -> (k p) r")).then_inc(e_ld[u], 16)
            for u in range(NU):
                sp.wait_ge(e_sc[u], NI * 16)
            for c in range(NX):
                sp.dma_start(g_all[:, c * CH:(c + 1) * CH, :], g_v[:, c * CH:(c + 1) * CH, :]).then_inc(g_in[c], 16)

            out_v = out.rearrange("(n j p) d -> n p j d", j=TB, p=P)
            with sp.Fori(0, NB) as i:
                sp.wait_ge(b_out.sem, b_out.at(i, 1))
                sp.dma_start(out_v[bass.ds(i, 1)].rearrange("n p j d -> (n p) j d"), obuf[:, :, :]).then_inc(out_done, 16)
            sp.wait_ge(out_done, 16 * (NB + 1))

        @block.gpsimd
        def _(pool):
            pool.sem_inc(b_ya.sem, 2)
            pool.sem_inc(b_fin.sem, 1)
            pool.sem_inc(b_gy.sem, 1)
            pool.sem_inc(out_done, 16)
            nc.gpsimd.memset(fill, 0.0)
            nc.gpsimd.iota(tid[:, :], pattern=[[P, NTILE]], base=0, channel_multiplier=1).then_inc(tid_ready, 1)
            nc.gpsimd.drain()
            nc.gpsimd.memset(fill[:, :, P:RW].bitcast(i32), NONE).then_inc(fill_ready, 1)

            def scatter(n, p):
                pool.wait_ge(a_xn.sem, a_xn.at(n, 1))
                pool.sem_inc(pool_turn, 1)
                for j in range(TB):
                    at = idx[p][:, j:j + 1] if p < 2 else pos_i[:, n * TB + j:n * TB + j + 1]
                    nc.gpsimd.indirect_dma_start(xs, bass.IndirectOffsetOnAxis(at, 0), xnrow[p][:, j, :], None).then_inc(a_scat[p % 2], 16)

            def add_bias(n):
                pool.wait_ge(a_se.sem, a_se.at(n, 1))
                nc.gpsimd.tensor_tensor(s_all[:, tiles(n), :], s_all[:, tiles(n), :], bo_bc.unsqueeze(1).to_broadcast([P, TB, P]), ALU.add).then_inc(a_bo.sem, 1)

            def differences(n, p, first=False):
                pool.wait_ge(a_xnT.sem, a_xnT.at(n, 1))
                if not first:
                    pool.wait_ge(a_mix.sem, a_mix.at(n, 0))
                nc.gpsimd.tensor_tensor(byseq(diff), xnT[p][:, :, 1:SEQ + 1], xnT[p][:, :, 0:SEQ], ALU.subtract).then_inc(a_d.sem, 1)

            differences(0, 0, first=True)
            pool.wait_ge(route_ready, 1)
            pool.wait_ge(fill_done, 16 * (NTL // 9))
            scatter(0, 2)
            differences(1, 1)
            scatter(1, 3)
            scatter(2, 0)
            differences(2, 0)
            scatter(3, 1)
            with pool.Fori(0, (NB - 4) // 2) as r:
                for p in (1, 0):
                    i = r * 2 + (2 - p)
                    differences(i + 2, p)
                    scatter(i + 3, 1 - p)
                    add_bias(i - 1)
            differences(NB - 1, 1)
            for n in range(NB - 4, NB):
                add_bias(n)

            with pool.Fori(0, NI) as i:
                for u in range(NU):
                    pool.wait_ge(e_g.sem, e_g.at(i * NU + u, 1))
                    pool.sem_inc(pool_turn, 1)
                    nc.gpsimd.indirect_dma_start(gs, bass.IndirectOffsetOnAxis(xsb[u][:, P:RW].bitcast(i32), 0), gout[u], None,
                                                 bounds_check=ntok - 1, oob_is_err=False).then_inc(e_sc[u], 16)

            for c in range(NX):
                pool.wait_ge(sg_ready, c + 1)
                c_ = slice(c * CH, (c + 1) * CH)
                nc.gpsimd.tensor_tensor(x_all[:, c_, :], x_all[:, c_, :], s_all[:, c_, :], ALU.add).then_inc(x1_ready, 1)

            def weigh_v(i, t, first):
                pool.wait_ge(b_a.sem, b_a.at(i, t + 1))
                s_, n = av_summed((t + 2) % TB)
                if t >= 2:
                    pool.wait_ge(s_.sem, s_.at(i, n))
                elif not first:
                    pool.wait_ge(s_.sem, s_.at(i, n - s_.per))
                a_b = A[t % 2].rearrange("p (h g) -> p g h", h=H).unsqueeze(3).to_broadcast([P, H, H, HD])
                v_b = kvs[:, t, :, HD:2 * HD].unsqueeze(2).to_broadcast([P, H, H, HD])
                nc.gpsimd.tensor_tensor(av[t % 2].rearrange("p (g h d) -> p g h d", g=H, h=H), a_b, v_b, ALU.mult).then_inc(b_av.sem, 1)

            def less_maxima(i, t):
                if t in POOL_MAX:
                    pool.wait_ge(b_mx.sem, b_mx.at(i, POOL_MAX.index(t) + 1))
                    s3 = S[t % 2].rearrange("p (h g) -> p h g", h=H)
                    nc.gpsimd.tensor_tensor(s3, s3, mx[t % 2].unsqueeze(2).to_broadcast([P, H, H]), ALU.subtract).then_inc(b_sc.sem, 1)

            def add_expert(i, p, e):
                if e == 0:
                    pool.wait_ge(b_yi.sem, b_yi.at(i, 1))
                else:
                    pool.wait_ge(b_ya.sem, b_ya.at(i, e))
                pool.wait_ge(b_ys.sem, b_ys.at(i, e + 1))
                nc.gpsimd.tensor_tensor(y[p], y[p], ysc[e % 2], ALU.add).then_inc(b_ya.sem, 1)

            def add_x(i, p):
                pool.wait_ge(b_th.sem, b_th.at(i, 1))
                nc.gpsimd.tensor_tensor(gy, th1, y[p], ALU.mult).then_inc(b_gy.sem, 1)
                pool.wait_ge(b_sp.sem, b_sp.at(i, 1))
                nc.gpsimd.tensor_tensor(byt(sp1), byt(sp1), hbp.unsqueeze(1).to_broadcast([P, TB, P]), ALU.add).then_inc(b_sb.sem, 1)
                pool.wait_ge(b_gy.sem, b_gy.at(i, 1))
                pool.wait_ge(b_sb.sem, b_sb.at(i, 1))
                nc.gpsimd.tensor_tensor(fin, sp1, gy, ALU.mult).then_inc(b_fin.sem, 1)
                pool.wait_ge(b_fin.sem, b_fin.at(i, 1))
                pool.wait_ge(out_done, i * 16 + 16)
                nc.gpsimd.tensor_tensor(obuf[:, :, :], byt(fin), x_all[:, tiles(i), :], ALU.add).then_inc(b_out.sem, 1)

            def layer1(i, p, first=False):
                less_maxima(i, 0)
                if not first:
                    add_expert(i - 1, 1 - p, 7)
                weigh_v(i, 0, first)
                add_expert(i, p, 0)
                for t in range(1, TB):
                    less_maxima(i, t)
                    add_expert(i, p, 2 * t - 1)
                    weigh_v(i, t, first)
                    add_expert(i, p, 2 * t)
                if not first:
                    add_x(i - 1, 1 - p)

            layer1(0, 0, first=True)
            with pool.Fori(0, (NB - 2) // 2) as r:
                layer1(r * 2 + 1, 1)
                layer1(r * 2 + 2, 0)
            layer1(NB - 1, 1)
            add_expert(NB - 1, 1, 7)
            add_x(NB - 1, 1)

        @block.scalar
        def _(act):
            av_ = nc.scalar.activation
            act.wait_ge(w_in, W_ALL)
            av_(ew[:, 0:1], col(C_W), ACT.Exp).then_inc(act_own, 1)
            act.wait_ge(act_own, 1)
            av_(ew[:, 1:2], ew[:, 0:1], ACT.Exp, scale=-1.0).then_inc(w_decay, 1)
            act.sem_inc(a_se.sem, 1)
            act.sem_inc(b_hs.sem, 2)
            act.sem_inc(b_ys.sem, 1)
            act.wait_ge(var_ready, 1)
            av_(rstd_all[:, :], mv_all[:, :, 1], ACT.Sqrt, bias=eps1[:, 0:1]).then_inc(sd_ready, 1)

            def copy_xnT(n, p):
                act.wait_ge(a_xT.sem, a_xT.at(n, 1))
                tp = banks[0][:, :].rearrange("p (b t) -> p b t", b=NSEQ)
                av_(xnT[p][:, :, 1:SEQ + 1], tp, ACT.Copy)
                av_(xnT[p][:, :, 0:1], tp[:, :, SEQ - 1:SEQ], ACT.Copy).then_inc(a_xnT.sem, 1)

            def values0(n):
                act.wait_ge(a_proj.sem, a_proj.at(n, 1))
                av_(v1, banks[1][:, :], ACT.Identity, bias=col(C_BV)).then_inc(a_v.sem, 1)

            def gate0(n, p):
                act.wait_ge(a_proj.sem, a_proj.at(n, 4))
                av_(th[p], banks[4][:, :], ACT.Tanh, bias=hbg[:, :], scale=0.5).then_inc(a_th.sem, 1)

            def out0(n):
                act.wait_ge(a_s.sem, a_s.at(n, 1))
                av_(s_all[:, tiles(n), :], byt(banks[6][:, :]), ACT.Copy).then_inc(a_se.sem, 1)

            def block0(i, p, first=False, left=3):
                if left >= 2:
                    copy_xnT(i + 2, p)
                act.wait_ge(a_c.sem, a_c.at(i, 1))
                av_(sq, banks[5][:, :], ACT.Square).then_inc(a_sq.sem, 1)
                act.wait_ge(a_vs.sem, a_vs.at(i, 1))
                av_(sd, vs, ACT.Sqrt, bias=eps1[:, 1:2], scale=4.0 / HD).then_inc(a_sd.sem, 1)
                if left >= 1:
                    values0(i + 1)
                if not first:
                    out0(i - 1)
                if left >= 1:
                    gate0(i + 1, 1 - p)

            copy_xnT(0, 0)
            copy_xnT(1, 1)
            values0(0)
            gate0(0, 0)
            block0(0, 0, first=True)
            with act.Fori(0, (NB - 4) // 2) as r:
                for p in (1, 0):
                    block0(r * 2 + (2 - p), p)
            for n in range(NB - 3, NB):
                block0(n, n % 2, left=NB - 1 - n)
            out0(NB - 1)

            def rows_T(k, b):
                act.wait_ge(e_T.sem, e_T.at(k, 1))
                av_(xsT[b], banks[0][:, b * P:(b + 1) * P], ACT.Copy).then_inc(e_xs.sem, 1)

            def tile0(k, u, first=False, last=False):
                b = u % 2
                act.wait_ge(e_h.sem, e_h.at(k, 1))
                for c in range(FC):
                    r = av_(hs[b][:, c, :], banks[2 + 2 * b][:, c * P:(c + 1) * P], ACT.Relu, bias=wc[b][:, 0, FF + c:FF + c + 1])
                r.then_inc(e_r0.sem, 1)
                if not last:
                    rows_T(k + 2, b)
                if not first:
                    act.wait_ge(e_yv.sem, e_yv.at(k - 1, 1))
                    av_(the[1 - b], ye[1 - b], ACT.Tanh, scale=0.5).then_inc(e_th.sem, 1)

            rows_T(0, 0)
            rows_T(1, 1)
            for u in range(NU):
                tile0(u, u, first=(u == 0))
            with act.Fori(1, NI - 1) as i:
                for u in range(NU):
                    tile0(i * NU + u, u)
            for u in range(NU):
                tile0(NTL - NU + u, u, last=(u >= NU - 2))
            act.wait_ge(e_yv.sem, e_yv.at(NTL - 1, 1))
            av_(the[1], ye[1], ACT.Tanh, scale=0.5).then_inc(e_th.sem, 1)

            def deviations1(t0, t1, n):
                act.wait_ge(var2_ready, n)
                av_(rstd_all[:, t0:t1], mv_all[:, t0:t1, 1], ACT.Sqrt, bias=eps1[:, 0:1]).then_inc(sd2_ready, 1)

            deviations1(0, CH, 1)

            def normalise1(i, first=False):
                if not first:
                    act.wait_ge(b_xT.sem, b_xT.at(i, 0))
                for j in range(TB):
                    t = tile_of(i, j)
                    r = av_(xn1[:, j, :], x_all[:, t, :], ACT.Identity, scale=rstd_all[:, t], bias=nmr_all[:, t])
                r.then_inc(b_xn.sem, 1)

            def copy_sp(i):
                act.wait_ge(b_s.sem, b_s.at(i, 1))
                act.wait_ge(b_fin.sem, b_fin.at(i, 0))
                av_(sp1, banks[3][:, :], ACT.Copy, scale=0.5).then_inc(b_sp.sem, 1)

            def relu_hidden(i, n, e, edge=False):
                k = hid(n, e, edge)
                act.wait_ge(b_h.sem, b_h.at(i, k))
                av_((h1s, h2s)[n - 1][e % 2][:, :], banks[4 + k % 2][:, :], ACT.Relu,
                    bias=col((C_LB1, C_LB2)[n - 1] + e)).then_inc(b_hs.sem, 1)

            def weigh_expert(i, p, e):
                act.wait_ge(b_y.sem, b_y.at(i, e + 1))
                act.wait_ge(b_ya.sem, b_ya.at(i, e - 1))
                for j in range(TB):
                    r = av_(ysc[e % 2][:, j * P:(j + 1) * P], banks[6][:, j * P:(j + 1) * P], ACT.Copy, scale=cw_[p][:, j, e:e + 1])
                r.then_inc(b_ys.sem, 1)

            def hidden_step(i, e, last=False):
                if e < E - 1:
                    relu_hidden(i, 1, e + 1)
                elif not last:
                    relu_hidden(i + 1, 1, 0)
                relu_hidden(i, 2, e, last)

            def expert_step(i, p, e, first=False, last=False):
                hidden_step(i, e, last)
                if e:
                    weigh_expert(i, p, e - 1)
                elif not first:
                    weigh_expert(i - 1, 1 - p, E - 1)

            def exps(i, t):
                act.wait_ge(b_sc.sem, b_sc.at(i, t + 1))
                av_(A[t % 2], S[t % 2], ACT.Exp, scale=0.125).then_inc(b_a.sem, 1)

            def copy_kv(i, t, first):
                act.wait_ge(b_qkvp.sem, b_qkvp.at(i, t + 1))
                if not first:
                    act.wait_ge(b_av.sem, b_av.at(i, t + 1 - TB))
                av_(kvs[:, t], banks[1 + t % 2][:, 0:3 * P].rearrange("p (h c) -> p h c", h=H)[:, :, HD:3 * HD], ACT.Copy).then_inc(b_kv.sem, 1)

            def copy_xT(i, p):
                act.wait_ge(b_xT.sem, b_xT.at(i, 1))
                av_(xT[p], banks[0][:, :], ACT.Copy).then_inc(b_xq.sem, 1)

            def copy_oT(i):
                act.wait_ge(b_oTp.sem, b_oTp.at(i, 1))
                av_(oT1, banks[0][:, :], ACT.Copy).then_inc(b_oT.sem, 1)

            def tanh1(i, p):
                act.wait_ge(b_ya.sem, b_ya.at(i, E))
                act.wait_ge(b_gy.sem, b_gy.at(i, 0))
                av_(th1, y[p], ACT.Tanh, scale=0.5).then_inc(b_tt.sem, 1)
                act.wait_ge(b_tt.sem, b_tt.at(i, 1))
                av_(th1, th1, ACT.Identity, bias=ones[:, 0:1]).then_inc(b_th.sem, 1)

            def start_y(i, p, first):
                act.wait_ge(b_y0.sem, b_y0.at(i, 1))
                if not first:
                    act.wait_ge(b_gy.sem, b_gy.at(i - 1, 0))
                av_(y[p], banks[3][:, :], ACT.Copy).then_inc(b_yi.sem, 1)

            def copy_wT(i):
                act.wait_ge(b_cwTp.sem, b_cwTp.at(i, 1))
                av_(wT[:, :], banks[3][0:E, :], ACT.Copy).then_inc(b_cwT.sem, 1)

            def exp_gate(i):
                act.wait_ge(b_lgs.sem, b_lgs.at(i, 1))
                av_(gw[1], gw[0], ACT.Exp).then_inc(b_ex.sem, 1)

            def layer1(i, p, first=False, last=False):
                copy_kv(i, 1, first)
                expert_step(i, p, 0, first)
                hidden_step(i, 1)
                copy_wT(i)
                weigh_expert(i, p, 0)
                exps(i, 0)
                start_y(i, p, first)
                copy_kv(i, 2, first)
                expert_step(i, p, 2)
                if not first:
                    tanh1(i - 1, 1 - p)
                    copy_oT(i - 1)
                if not last:
                    normalise1(i + 1)
                exps(i, 1)
                expert_step(i, p, 3)
                copy_kv(i, 3, first)
                if not last:
                    copy_xT(i + 1, 1 - p)
                expert_step(i, p, 4)
                exps(i, 2)
                if not first:
                    copy_sp(i - 1)
                expert_step(i, p, 5)
                if not last:
                    copy_kv(i + 1, 0, False)
                    exp_gate(i + 1)
                expert_step(i, p, 6)
                exps(i, 3)
                expert_step(i, p, 7, last=last)

            act.wait_ge(norm_ready, 1)
            normalise1(0, True)
            copy_xT(0, 0)
            copy_kv(0, 0, True)
            relu_hidden(0, 1, 0, edge=True)
            deviations1(CH, NTILE, 2)
            act.wait_ge(norm_ready, 2)
            exp_gate(0)
            layer1(0, 0, first=True)
            with act.Fori(0, (NB - 2) // 2) as r:
                layer1(r * 2 + 1, 1)
                layer1(r * 2 + 2, 0)
            layer1(NB - 1, 1, last=True)
            weigh_expert(NB - 1, 1, E - 1)
            tanh1(NB - 1, 1)
            copy_oT(NB - 1)
            copy_sp(NB - 1)

        @block.vector
        def _(dve):
            own = Chain(dve, dve_own)
            link, add = own.link, own.add
            v = nc.vector
            dve.sem_inc(e_yv.sem, 2)
            v.memset(eps1[:, 0:1], EPS)
            v.memset(eps1[:, 1:2], 4 * EPS)
            link(v.memset(ones[:, :], 1.0))
            def stats(c):
                for t in range(c * CH, (c + 1) * CH):
                    v.bn_stats(st_all[:, t, :], x_all[:, t, :])

            def mean_var(t0, t1):
                me, qe, mo, qo = (st_all[:, t0:t1, n] for n in (1, 2, 4, 5))
                mean, var = mv_all[:, t0:t1, 0], mv_all[:, t0:t1, 1]
                link(v.tensor_tensor(mean, me, mo, ALU.subtract))
                link(v.scalar_tensor_tensor(var, mean, 0.25 * P, mean, ALU.mult, ALU.mult))
                link(v.tensor_tensor(var, var, qe, ALU.add))
                link(v.tensor_tensor(var, var, qo, ALU.add))
                link(v.tensor_scalar(var, var, 1.0 / P, None, ALU.mult))
                link(v.tensor_tensor(mean, me, mo, ALU.add))
                link(v.tensor_scalar(mean, mean, 0.5, None, ALU.mult))

            for c in range(NX):
                dve.wait_ge(x_in[c], 16)
                stats(c)
            dve.drain()
            mean_var(0, NTILE)
            dve.sem_inc(var_ready, 1)
            dve.wait_ge(sd_ready, 1)
            link(v.reciprocal(rstd_all[:, :], rstd_all[:, :]))

            def weights0():
                dve.wait_ge(w_in, W_ALL)
                dve.wait_ge(w_decay, 1)
                v.tensor_scalar(decay[:, :], ones[:, :], ew[:, 1:2], None, ALU.mult)
                v.tensor_scalar(hbg[:, :], col(C_BG), 0.5, None, ALU.mult)
                link(v.tensor_scalar(omm[:, :], cols_sb[:, C_MIX:C_MIX + 4], -1.0, 1.0, ALU.mult, ALU.add))
                for n in range(4):
                    if n in MIXED:
                        continue
                    v.tensor_scalar(wm[:, n, 0, :], w4_sb[:, n, :], col(C_MIX + n), None, ALU.mult)
                    r = v.tensor_scalar(wm[:, n, 1, :], w4_sb[:, n, :], omm[:, n:n + 1], None, ALU.mult)
                r.then_inc(wm_ready, 1)

            def last_biases0():
                link(v.tensor_tensor(b2p[:, :, :], b2_bc[:, 0:E, :], b2_bc[:, 1:E + 1, :], ALU.add))
                link(v.tensor_scalar(b2p[:, :, :], b2p[:, :, :], 0.5, None, ALU.mult))

            def routing():
                wide = [P, NTILE, 2]
                link(v.tensor_tensor(x01, x_all[:, :, 0:2], mv_all[:, :, 0:1].to_broadcast(wide), ALU.subtract))
                link(v.tensor_tensor(x01, x01, rstd_all[:, :].unsqueeze(2).to_broadcast(wide), ALU.mult))
                c_sum, c_abs, c_fl, c_gt, c_sg, c_0 = cls[0:6]
                link(v.tensor_tensor(c_sum, x01[:, :, 0], x01[:, :, 1], ALU.add))
                link(v.tensor_scalar(c_sg, c_sum, 0.0, None, ALU.is_ge))
                link(v.tensor_scalar(c_sg, c_sg, 2.0, -1.0, ALU.mult, ALU.add))
                link(v.tensor_tensor(c_abs, c_sum, c_sg, ALU.mult))
                link(v.tensor_copy(clsi[0], c_abs))
                link(v.tensor_copy(c_fl, clsi[0]))
                link(v.tensor_tensor(c_gt, c_fl, c_abs, ALU.is_gt))
                link(v.tensor_tensor(c_fl, c_fl, c_gt, ALU.subtract))
                link(v.tensor_tensor(clsi[0], c_fl, c_sg, ALU.mult))
                link(v.tensor_scalar(clsi[1], clsi[0], 7, None, ALU.bitwise_and))
                link(v.tensor_copy(c_0, clsi[1]))
                full = [P, NTILE, E]
                v.tensor_tensor(oh3, iota.unsqueeze(1).to_broadcast(full), c_0.unsqueeze(2).to_broadcast(full), ALU.is_equal).then_inc(onehot_ready, 1)
                weights0()
                dve.wait_ge(tid_ready, 1)
                rows0(0, 2, None)
                rows0(1, 3, None)
                dve.wait_ge(counts_done, 1)
                before = banks[5][:, :].rearrange("p (n c) -> p n c", c=E)
                total = banks[6][:, :].rearrange("p (n c) -> p n c", c=E)
                for c in range(E):
                    last = v.tensor_tensor_scan(cum[:, c, :], ones[:, 0:NTILE], total[:, :, c], 0.0, ALU.mult, ALU.add)
                link(last)
                n_, nt, end, base = ncl
                link(v.tensor_scalar(ncli, cum[:, :, NTILE - 1], float(P - 1), None, ALU.add))
                link(v.tensor_scalar(ncli, ncli, P.bit_length() - 1, None, ALU.logical_shift_right))
                link(v.tensor_copy(nt, ncli))
                link(v.tensor_tensor_scan(end, ones[:, 0:E], nt, 0.0, ALU.mult, ALU.add))
                link(v.tensor_tensor(base, end, nt, ALU.subtract))
                link(v.tensor_scalar(base, base, float(P), None, ALU.mult))
                link(v.tensor_tensor(off, cum.rearrange("p c n -> p n c"), total, ALU.subtract))
                link(v.tensor_tensor(off, off, before, ALU.add))
                link(v.tensor_tensor(off, off, base.unsqueeze(1).to_broadcast(full), ALU.add))
                link(v.tensor_tensor(off, off, oh3, ALU.mult))
                link(v.tensor_reduce(posf, off, X, ALU.add))
                link(v.tensor_copy(pos_i[:, :], posf))
                every = [P, NTL, E]
                link(v.tensor_tensor(tcmp, end.unsqueeze(1).to_broadcast(every), tile_no.unsqueeze(2).to_broadcast(every), ALU.is_le))
                link(v.tensor_reduce(tcf, tcmp, X, ALU.add))
                link(v.tensor_scalar(tcls[:, :], tcf, float(E - 1), None, ALU.min))
                dve.sem_inc(route_ready, 1)

            def rows0(n, p, before):
                if before is not None:
                    dve.wait_ge(a_scat[p], before * (16 * TB))
                    dve.wait_ge(a_xT.sem, a_xT.at(n - 1, 0))
                if p < 2:
                    link(v.tensor_copy(idx[p], pos_i[:, tiles(n)]))
                v.tensor_copy(xnrow[p][:, :, P:RW].bitcast(i32), tid[:, tiles(n)].unsqueeze(2))
                for j in range(TB):
                    t = tile_of(n, j)
                    last = v.tensor_scalar(xnrow[p][:, j, 0:P], x_all[:, t, :], mv_all[:, t, 0], rstd_all[:, t], ALU.subtract, ALU.mult)
                last.then_inc(a_xn.sem, 1)

            def kv0(n):
                dve.wait_ge(a_v.sem, a_v.at(n, 1))
                dve.wait_ge(a_proj.sem, a_proj.at(n, 2))
                link(v.scalar_tensor_tensor(kv, banks[2][:, :], col(C_BK), v1, ALU.add, ALU.mult))

            def wkv0(n):
                for b in range(NSEQ):
                    s_ = slice(b * SEQ, (b + 1) * SEQ)
                    last = v.tensor_tensor_scan(acc[:, s_], decay[:, :], kv[:, s_], 0.0, ALU.mult, ALU.add)
                link(last)
                link(v.scalar_tensor_tensor(wkv, kv, col(C_U), acc, ALU.mult, ALU.add))
                dve.wait_ge(a_proj.sem, a_proj.at(n, 3))
                v.scalar_tensor_tensor(rw, banks[3][:, :], col(C_BR), wkv, ALU.add, ALU.mult).then_inc(a_rw.sem, 1)

            def mix0(n, p):
                dve.wait_ge(a_d.sem, a_d.at(n, 1))
                for m in MIXED:
                    last = v.scalar_tensor_tensor(byseq(mix[m][p]), byseq(diff), col(C_MIX + m), xnT[p][:, :, 0:SEQ], ALU.mult, ALU.add)
                last.then_inc(a_mix.sem, 1)

            def block0(i, p, before, first=False, left=3):
                dve.wait_ge(a_sq.sem, a_sq.at(i, 1))
                v.tensor_reduce(vs, sq.rearrange("p (h d) -> p h d", d=HD), X, ALU.add).then_inc(a_vs.sem, 1)
                if left >= 3:
                    rows0(i + 3, 1 - p, before)
                dve.wait_ge(a_sd.sem, a_sd.at(i, 1))
                link(v.reciprocal(rh, sd))
                v.tensor_tensor(o.rearrange("p (h d) -> p h d", d=HD), banks[5][:, :].rearrange("p (h d) -> p h d", d=HD),
                                rh.unsqueeze(2).to_broadcast([P, TB * H, HD]), ALU.mult).then_inc(a_o.sem, 1)
                if left >= 1:
                    kv0(i + 1)
                    wkv0(i + 1)
                dve.wait_ge(a_oTp.sem, a_oTp.at(i, 1))
                dve.wait_ge(a_th.sem, a_th.at(i, 1))
                v.scalar_tensor_tensor(oT, th[p], 1.0, banks[7][:, :], ALU.add, ALU.mult).then_inc(a_oT.sem, 1)
                if left >= 2:
                    dve.wait_ge(a_proj.sem, a_proj.at(i, 4))
                    mix0(i + 2, p)

            routing()
            mix0(0, 0)
            kv0(0)
            wkv0(0)
            rows0(2, 0, None)
            mix0(1, 1)
            block0(0, 0, None, first=True)
            with dve.Fori(0, (NB - 4) // 2) as r:
                own.enter(r, 2 * 5)
                for p in (1, 0):
                    block0(r * 2 + (2 - p), p, r + 2)
            own.leave((NB - 4) // 2)
            for n in range(NB - 3, NB):
                block0(n, n % 2, None, left=NB - 1 - n)

            def class_weights(k, b):
                c = dve.value_load(tcls[0:1, bass.ds(k, 1)], min_val=0, max_val=E - 1)
                v.tensor_copy(wc[b], w1x[:, bass.ds(c, 2), :]).then_inc(e_wc.sem, 1)

            def outputs0(k, b):
                c = dve.value_load(tcls[0:1, bass.ds(k, 1)], min_val=0, max_val=E - 1)
                dve.wait_ge(e_y.sem, e_y.at(k, 1))
                v.scalar_tensor_tensor(ye[b].unsqueeze(1), banks[6 + b][:, 0:P].unsqueeze(1), 0.5, b2p[:, bass.ds(c, 1), :], ALU.mult, ALU.add).then_inc(e_yv.sem, 1)

            def silu0(k, u):
                b = u % 2
                dve.wait_ge(e_th.sem, e_th.at(k, 1))
                v.scalar_tensor_tensor(gout[u], the[b], 1.0, ye[b], ALU.add, ALU.mult).then_inc(e_g.sem, 1)

            def tile0(k, u, first=False, copy=True):
                b = u % 2
                dve.wait_ge(e_h.sem, e_h.at(k, 2))
                for c in range(FC):
                    r = v.tensor_scalar(hs[b][:, FC + c, :], banks[3 + 2 * b][:, c * P:(c + 1) * P], wc[b][:, 1, FF + c:FF + c + 1], 0.0, ALU.add, ALU.max)
                r.then_inc(e_r1.sem, 1)
                if not first:
                    outputs0(k - 1, 1 - b)
                if copy:
                    dve.wait_ge(e_r0.sem, e_r0.at(k, 1))
                    dve.wait_ge(e_r1.sem, e_r1.at(k, 1))
                    class_weights(k + 2, b)
                if not first:
                    silu0(k - 1, (u - 1) % NU)

            last_biases0()
            dve.wait_ge(we_in, WE_ALL)
            dve.wait_ge(a_se.sem, a_se.at(NB, 0))
            for p in range(2):
                dve.wait_ge(a_scat[p], NB // 2 * 16 * TB)
            class_weights(0, 0)
            class_weights(1, 1)
            for u in range(NU):
                tile0(u, u, first=(u == 0))
            with dve.Fori(1, NI - 1) as i:
                for u in range(NU):
                    tile0(i * NU + u, u)
            for u in range(NU):
                tile0(NTL - NU + u, u, copy=(u < NU - 2))
            outputs0(NTL - 1, 1)
            silu0(NTL - 1, NU - 1)

            dve.wait_ge(a_bo.sem, a_bo.at(NB, 0))
            for c in range(NX):
                c_ = slice(c * CH, (c + 1) * CH)
                dve.wait_ge(g_in[c], 16)
                v.scalar_tensor_tensor(s_all[:, c_, :], s_all[:, c_, :], 0.5, g_all[:, c_, :], ALU.mult, ALU.mult).then_inc(sg_ready, 1)
            def norms1(t0, t1, n):
                t_ = slice(t0, t1)
                mean_var(t0, t1)
                dve.sem_inc(var2_ready, 1)
                dve.wait_ge(sd2_ready, n)
                link(v.reciprocal(rstd_all[:, t_], rstd_all[:, t_]))
                v.scalar_tensor_tensor(nmr_all[:, t_], mv_all[:, t_, 0], -1.0, rstd_all[:, t_], ALU.mult, ALU.mult).then_inc(norm_ready, 1)

            v.tensor_scalar(hbp[:, :], bp_bc, 0.5, None, ALU.mult)
            dve.wait_ge(x1_ready, 1)
            stats(0)
            dve.drain()
            norms1(0, CH, 1)
            for c in range(1, NX):
                dve.wait_ge(x1_ready, c + 1)
                stats(c)
            dve.drain()

            own_at = {}

            def product(i, t):
                dve.wait_ge(b_kv.sem, b_kv.at(i, t + 1))
                q_b = banks[1 + t % 2][:, 0:3 * P].rearrange("p (h c) -> p h c", h=H)[:, :, 0:HD].unsqueeze(2).to_broadcast([P, H, H, HD])
                k_b = kvs[:, t, :, 0:HD].unsqueeze(1).to_broadcast([P, H, H, HD])
                v.tensor_tensor(prod.rearrange("p (h g d) -> p h g d", h=H, g=H), q_b, k_b, ALU.mult).then_inc(b_qk.sem, 1)

            def scores(i, t):
                dve.wait_ge(b_qk.sem, b_qk.at(i, t + 1))
                own_at["scores"] = own.add(v.tensor_reduce(S[t % 2], prod.rearrange("p (s d) -> p s d", d=HD), X, ALU.add))

            def maxima(i, t):
                dve.wait_ge(dve_own, own_at["scores"])
                r = v.tensor_reduce(mx[t % 2], S[t % 2].rearrange("p (h g) -> p h g", h=H), X, ALU.max)
                if t in POOL_MAX:
                    r.then_inc(b_mx.sem, 1)
                else:
                    own_at["maxima"] = own.add(r)

            def less_maxima(i, t):
                if t in POOL_MAX:
                    return
                dve.wait_ge(dve_own, own_at["maxima"])
                s3 = S[t % 2].rearrange("p (h g) -> p h g", h=H)
                v.tensor_tensor(s3, s3, mx[t % 2].unsqueeze(2).to_broadcast([P, H, H]), ALU.subtract).then_inc(b_sc.sem, 1)

            def denominators(i, t):
                dve.wait_ge(b_a.sem, b_a.at(i, t + 1))
                own_at["den"] = own.add(v.tensor_reduce(den[:, t * H:(t + 1) * H], A[t % 2].rearrange("p (h g) -> p h g", h=H), X, ALU.add))

            def inverses(i, t):
                dve.wait_ge(dve_own, own_at["den"])
                own_at["rden"] = own.add(v.reciprocal(rden[:, t * H:(t + 1) * H], den[:, t * H:(t + 1) * H]))

            def sum_av(i, t):
                if t not in PE_AV:
                    dve.wait_ge(b_av.sem, b_av.at(i, t + 1))
                    v.tensor_reduce(red, av[t % 2].rearrange("p (g o) -> p o g", g=H), X, ALU.add).then_inc(b_avr.sem, 1)

            def heads_out(i, t):
                s_, n = av_summed(t)
                dve.wait_ge(s_.sem, s_.at(i, n))
                src = banks[7][:, t * P:(t + 1) * P] if t in PE_AV else red
                v.tensor_tensor(o1[:, t * P:(t + 1) * P].rearrange("p (h d) -> p h d", d=HD), src.rearrange("p (h d) -> p h d", d=HD),
                                rden[:, t * H:(t + 1) * H].unsqueeze(2).to_broadcast([P, H, HD]), ALU.mult).then_inc(b_of.sem, 1)

            lg, ex, first_, second, low, eq = gw
            m_, r_, z_, z2 = sm
            rv = rev.unsqueeze(1).to_broadcast([P, TB, E])

            def b_(a):
                return a.unsqueeze(2).to_broadcast([P, TB, E])

            def logits(i):
                dve.wait_ge(b_lg.sem, b_lg.at(i, 1))
                own_at["lg"] = own.add(v.tensor_tensor(lg, banks[0][:, 0:TB * E].rearrange("p (j e) -> p j e", j=TB),
                                                       gateb_bc.unsqueeze(1).to_broadcast([P, TB, E]), ALU.add))

            def max_logit():
                dve.wait_ge(dve_own, own_at["lg"])
                own_at["m"] = own.add(v.tensor_reduce(m_, lg, X, ALU.max))

            def less_max_logit():
                dve.wait_ge(dve_own, own_at["m"])
                v.tensor_tensor(lg, lg, b_(m_), ALU.subtract).then_inc(b_lgs.sem, 1)

            def first_1(i):
                dve.wait_ge(b_lgs.sem, b_lgs.at(i, 1))
                own_at["f1"] = own.add(v.scalar_tensor_tensor(eq, lg, 0.0, rv, ALU.is_equal, ALU.mult))

            def first_2():
                dve.wait_ge(dve_own, own_at["f1"])
                own_at["f2"] = own.add(v.tensor_reduce(r_, eq, X, ALU.max))

            def first_3():
                dve.wait_ge(dve_own, own_at["f2"])
                own_at["f3"] = own.add(v.tensor_tensor(first_, rv, b_(r_), ALU.is_equal))

            def second_1(i):
                dve.wait_ge(dve_own, own_at["f3"])
                dve.wait_ge(b_ex.sem, b_ex.at(i, 1))
                own_at["s1"] = own.add(v.scalar_tensor_tensor(low, first_, -2.0, ex, ALU.mult, ALU.add))

            def second_2():
                dve.wait_ge(dve_own, own_at["s1"])
                own_at["s2"] = own.add(v.tensor_reduce(m_, low, X, ALU.max))

            def second_3():
                dve.wait_ge(dve_own, own_at["s2"])
                own_at["s3"] = own.add(v.tensor_tensor(eq, low, b_(m_), ALU.is_equal))

            def second_4():
                dve.wait_ge(dve_own, own_at["s3"])
                own_at["s4"] = own.add(v.tensor_tensor(eq, eq, rv, ALU.mult))

            def second_5():
                dve.wait_ge(dve_own, own_at["s4"])
                own_at["s5"] = own.add(v.tensor_reduce(r_, eq, X, ALU.max))

            def second_6():
                dve.wait_ge(dve_own, own_at["s5"])
                own_at["s6"] = own.add(v.tensor_tensor(second, rv, b_(r_), ALU.is_equal))

            def exp_sum():
                own_at["z"] = own.add(v.tensor_reduce(z_, ex, X, ALU.add))

            def inverse_exp_sum():
                dve.wait_ge(dve_own, own_at["z"])
                own_at["z2"] = own.add(v.reciprocal(z2, z_))

            def probabilities():
                dve.wait_ge(dve_own, own_at["z2"])
                own_at["p01"] = own.add(v.tensor_tensor(p01, ex[:, :, 0:2], z2.unsqueeze(2).to_broadcast([P, TB, 2]), ALU.mult))

            def first_weight():
                dve.wait_ge(dve_own, own_at["p01"])
                v.tensor_tensor(first_, first_, b_(p01[:, :, 0]), ALU.mult)

            def second_weight():
                dve.wait_ge(dve_own, own_at["s6"])
                own_at["w"] = own.add(v.tensor_tensor(second, second, b_(p01[:, :, 1]), ALU.mult))

            def expert_weights(i, p, first=False):
                if not first:
                    dve.wait_ge(b_ys.sem, b_ys.at(i, -E))
                dve.wait_ge(dve_own, own_at["w"])
                v.tensor_tensor(cw_[p], first_, second, ALU.add).then_inc(b_cw.sem, 1)

            def route(i, p, first=False):
                first_1(i)
                first_2()
                first_3()
                second_1(i)
                exp_sum()
                second_2()
                inverse_exp_sum()
                second_3()
                probabilities()
                second_4()
                first_weight()
                second_5()
                second_6()
                second_weight()
                expert_weights(i, p, first)

            def layer1(i, p, first=False, last=False):
                if not first:
                    sum_av(i - 1, 2)
                product(i, 0)
                if not first:
                    heads_out(i - 1, 2)
                    denominators(i - 1, 3)
                scores(i, 0)
                if not first:
                    inverses(i - 1, 3)
                maxima(i, 0)
                less_maxima(i, 0)

                if not first:
                    sum_av(i - 1, 3)
                product(i, 1)
                if not first:
                    heads_out(i - 1, 3)
                denominators(i, 0)
                scores(i, 1)
                inverses(i, 0)
                maxima(i, 1)
                less_maxima(i, 1)

                if not first:
                    dve.wait_ge(b_oTp.sem, b_oTp.at(i - 1, 1))
                sum_av(i, 0)
                product(i, 2)
                heads_out(i, 0)
                denominators(i, 1)
                scores(i, 2)
                inverses(i, 1)
                maxima(i, 2)
                less_maxima(i, 2)

                sum_av(i, 1)
                if not last:
                    logits(i + 1)
                heads_out(i, 1)
                if not last:
                    max_logit()
                product(i, 3)
                if not last:
                    less_max_logit()
                denominators(i, 2)
                scores(i, 3)
                if not last:
                    first_1(i + 1)
                maxima(i, 3)
                if not last:
                    first_2()
                less_maxima(i, 3)
                if not last:
                    first_3()
                inverses(i, 2)
                if not last:
                    second_1(i + 1)
                    exp_sum()
                    second_2()
                    inverse_exp_sum()
                    second_3()
                    probabilities()
                    second_4()
                    first_weight()
                    second_5()
                    second_6()
                    second_weight()
                    expert_weights(i + 1, 1 - p, first)

            logits(0)
            max_logit()
            less_max_logit()
            norms1(CH, NTILE, 2)
            route(0, 0, True)
            layer1(0, 0, first=True)
            with dve.Fori(0, (NB - 2) // 2) as r:
                own.enter(r, 2 * (4 * TB + 15 - len(POOL_MAX)))
                layer1(r * 2 + 1, 1)
                layer1(r * 2 + 2, 0)
            own.leave((NB - 2) // 2)
            layer1(NB - 1, 1, last=True)
            sum_av(NB - 1, 2)
            denominators(NB - 1, 3)
            dve.wait_ge(dve_own, own_at["rden"])
            heads_out(NB - 1, 2)
            inverses(NB - 1, 3)
            sum_av(NB - 1, 3)
            dve.wait_ge(dve_own, own_at["rden"])
            heads_out(NB - 1, 3)

        @block.tensor
        def _(pe):
            mm = nc.tensor.matmul

            def tr(src, done, dst=0):
                for j in range(TB):
                    last = nc.tensor.transpose(banks[dst][:, j * P:(j + 1) * P], src[:, j, :], ident[:, :])
                last.then_inc(done.sem, 1)

            def token_major(dst, src, rhs, done):
                for j in range(TB):
                    last = mm(dst[:, j * P:(j + 1) * P], src[:, j * P:(j + 1) * P], rhs, start=True, stop=True)
                last.then_inc(done.sem, 1)

            pe.wait_ge(w_in, W_ALL)
            pe.wait_ge(onehot_ready, 1)
            mm(banks[5][:, :], below[:, :], onehot, start=True, stop=True)
            mm(banks[6][:, :], ones[:, 0:P], onehot, start=True, stop=True).then_inc(counts_done, 1)

            def rows_T0(n, p):
                pe.wait_ge(a_xn.sem, a_xn.at(n, 1))
                tr(xnrow[p][:, :, 0:P], a_xT)

            def project0(n, p, first=False):
                pe.wait_ge(a_xnT.sem, a_xnT.at(n, 1))
                for m, b in ((V_, 1), (K_, 2), (R_, 3), (G_, 4)):
                    dst = banks[b][:, :].rearrange("p (b t) -> p b t", b=NSEQ)
                    if m == G_ and not first:
                        pe.wait_ge(a_th.sem, a_th.at(n, 0))
                    if m in MIXED:
                        pe.wait_ge(a_mix.sem, a_mix.at(n, 1))
                        mm(dst, w4_sb[:, m, :], byseq(mix[m][p]), start=True, stop=True).then_inc(a_proj.sem, 1)
                    else:
                        mm(dst, wm[:, m, 0, :], xnT[p][:, :, 1:SEQ + 1], start=True, stop=False)
                        mm(dst, wm[:, m, 1, :], xnT[p][:, :, 0:SEQ], start=False, stop=True).then_inc(a_proj.sem, 1)

            def out_w0(n):
                pe.wait_ge(a_oT.sem, a_oT.at(n, 1))
                pe.wait_ge(a_se.sem, a_se.at(n, 0))
                token_major(banks[6], oT, wo_sb[:, :], a_s)

            def block0(i, p, first=False, left=3):
                if left >= 2:
                    pe.wait_ge(a_xnT.sem, a_xnT.at(i + 1, 1))
                    rows_T0(i + 2, p)
                pe.wait_ge(a_rw.sem, a_rw.at(i, 1))
                token_major(banks[5], rw, center[:, :], a_c)
                if not first:
                    out_w0(i - 1)
                if left >= 1:
                    project0(i + 1, 1 - p)
                pe.wait_ge(a_o.sem, a_o.at(i, 1))
                tr(byt(o), a_oTp, 7)

            pe.wait_ge(wm_ready, 1)
            rows_T0(0, 2)
            pe.wait_ge(a_xnT.sem, a_xnT.at(0, 1))
            rows_T0(1, 3)
            project0(0, 0, first=True)
            block0(0, 0, first=True)
            with pe.Fori(0, (NB - 4) // 2) as r:
                for p in (1, 0):
                    block0(r * 2 + (2 - p), p)
            for n in range(NB - 3, NB):
                block0(n, n % 2, left=NB - 1 - n)
            out_w0(NB - 1)

            def rows_T1(k, ku, loads):
                pe.wait_ge(e_ld[ku], loads * 16)
                b = ku % 2
                nc.tensor.transpose(banks[0][:, b * P:(b + 1) * P], xsb[ku][:, 0:P], ident[:, :]).then_inc(e_T.sem, 1)

            def hidden0(k, ku):
                b = ku % 2
                pe.wait_ge(e_xs.sem, e_xs.at(k, 1))
                pe.wait_ge(e_wc.sem, e_wc.at(k, 1))
                for e in range(2):
                    for c in range(FC):
                        last = mm(banks[2 + 2 * b + e][:, c * P:(c + 1) * P], wc[b][:, e, c * P:(c + 1) * P], xsT[b], start=True, stop=True)
                    last.then_inc(e_h.sem, 1)

            def out0(k, u):
                b = u % 2
                cl = pe.value_load(tcls[0:1, bass.ds(k, 1)], min_val=0, max_val=E - 1)
                pe.wait_ge(e_yv.sem, e_yv.at(k, -1))
                for e in range(2):
                    pe.wait_ge((e_r0, e_r1)[e].sem, (e_r0, e_r1)[e].at(k, 1))
                    for c in range(FC):
                        n = e * FC + c
                        last = mm(banks[6 + b][:, 0:P], hs[b][:, n, :], w2x[:, bass.ds(cl + e, 1), c, :],
                                  start=(n == 0), stop=(n == 2 * FC - 1))
                last.then_inc(e_y.sem, 1)

            pe.wait_ge(we_in, WE_ALL)
            def tile0(k, u, loads, left=2):
                if left >= 1:
                    hidden0(k + 1, (u + 1) % NU)
                if left >= 2:
                    rows_T1(k + 2, (u + 2) % NU, loads + (u + 2) // NU)
                out0(k, u)

            rows_T1(0, 0, 1)
            pe.wait_ge(e_xs.sem, e_xs.at(0, 1))
            rows_T1(1, 1, 1)
            hidden0(0, 0)
            for u in range(NU):
                tile0(u, u, 1)
            with pe.Fori(1, NI - 1) as i:
                for u in range(NU):
                    tile0(i * NU + u, u, i + 1)
            for u in range(NU):
                tile0(NTL - NU + u, u, NI, NU - 1 - u)

            def hidden1(i, p, n, e, edge=False):
                k = hid(n, e, edge)
                pe.wait_ge(b_hs.sem, b_hs.at(i, k - 2))
                mm(banks[4 + k % 2][:, :], l_sb[n - 1][:, e, :], xT[p] if n == 1 else h1s[e % 2], start=True, stop=True).then_inc(b_h.sem, 1)

            def out1(i, e, last=False):
                pe.wait_ge(b_hs.sem, b_hs.at(i, hid(2, e, last)))
                pe.wait_ge(b_ys.sem, b_ys.at(i, e))
                token_major(banks[6], h2s[e % 2], l_sb[2][:, e, :], b_y)

            def hidden_step(i, p, e, last=False):
                if e < E - 1:
                    hidden1(i, p, 1, e + 1)
                elif not last:
                    hidden1(i + 1, 1 - p, 1, 0)
                hidden1(i, p, 2, e, last)

            def expert_step(i, p, e, first=False, last=False):
                hidden_step(i, p, e, last)
                if e:
                    out1(i, e - 1)
                elif not first:
                    out1(i - 1, E - 1)

            def qkv1(i, p, t, first=False):
                if not first:
                    pe.wait_ge(b_qk.sem, b_qk.at(i, t - 1))
                mm(banks[1 + t % 2][:, 0:3 * P], xT[p][:, t * P:(t + 1) * P], wqkv_sb[:, :], start=True, stop=True).then_inc(b_qkvp.sem, 1)

            def gate1(i, p):
                pe.wait_ge(b_xq.sem, b_xq.at(i, 1))
                for j in range(TB):
                    last = mm(banks[0][:, j * E:(j + 1) * E], xT[p][:, j * P:(j + 1) * P], gate_sb[:, :], start=True, stop=True)
                last.then_inc(b_lg.sem, 1)

            def next_T(i):
                pe.wait_ge(b_xn.sem, b_xn.at(i, 1))
                tr(xn1, b_xT)

            def sum_heads(i, t, first=False):
                if t not in PE_AV:
                    return
                pe.wait_ge(b_av.sem, b_av.at(i, t + 1))
                if not (first and t == 0):
                    pe.wait_ge(b_of.sem, b_of.at(i, t))
                for g in range(H):
                    last = mm(banks[7][:, t * P:(t + 1) * P], ident[:, :], av[t % 2][:, g * P:(g + 1) * P], start=(g == 0), stop=(g == H - 1))
                last.then_inc(b_avp.sem, 1)

            def heads_T(i):
                pe.wait_ge(b_of.sem, b_of.at(i + 1, 0))
                tr(byt(o1), b_oTp)

            def project(i):
                pe.wait_ge(b_oT.sem, b_oT.at(i, 1))
                token_major(banks[3], oT1, wproj_sb[:, :], b_s)

            def weights_T(i, p):
                pe.wait_ge(b_cw.sem, b_cw.at(i, 1))
                for j in range(TB):
                    r = nc.tensor.transpose(banks[3][0:E, j * P:(j + 1) * P], cw_[p][:, j, :], ident[:, :])
                r.then_inc(b_cwTp.sem, 1)

            def biases(i):
                pe.wait_ge(b_cwT.sem, b_cwT.at(i, 1))
                token_major(banks[3], wT, b3_sb[:, :], b_y0)

            def layer1(i, p, first=False, last=False):
                qkv1(i, p, 1, first)
                expert_step(i, p, 0, first)
                if not first:
                    sum_heads(i - 1, 3)
                hidden_step(i, p, 1)
                weights_T(i, p)
                out1(i, 0)
                qkv1(i, p, 2)
                biases(i)
                expert_step(i, p, 2)
                if not first:
                    heads_T(i - 1)
                sum_heads(i, 0, first)
                expert_step(i, p, 3)
                qkv1(i, p, 3)
                if not last:
                    if not first:
                        pe.wait_ge(b_oT.sem, b_oT.at(i - 1, 1))
                    next_T(i + 1)
                expert_step(i, p, 4)
                if not last:
                    gate1(i + 1, 1 - p)
                sum_heads(i, 1)
                if not first:
                    project(i - 1)
                expert_step(i, p, 5)
                if not last:
                    qkv1(i + 1, 1 - p, 0)
                expert_step(i, p, 6)
                sum_heads(i, 2)
                expert_step(i, p, 7, last=last)

            pe.wait_ge(wb_in, WB_ALL)
            next_T(0)
            gate1(0, 0)
            qkv1(0, 0, 0, True)
            hidden1(0, 0, 1, 0, edge=True)
            layer1(0, 0, first=True)
            with pe.Fori(0, (NB - 2) // 2) as r:
                layer1(r * 2 + 1, 1)
                layer1(r * 2 + 2, 0)
            layer1(NB - 1, 1, last=True)
            out1(NB - 1, E - 1, last=True)
            sum_heads(NB - 1, 3)
            heads_T(NB - 1)
            project(NB - 1)


def kernel(**inputs):
    import numpy as _np
    import concourse.bacc as _bacc
    from concourse import mybir as _mybir
    from concourse.bass_utils import run_bass_kernel_spmd as _run

    a = {k: _np.asarray(v) for k, v in inputs.items()}
    x = a["L0_attn_x"]
    c = _np.ascontiguousarray
    names = ["mg", "mr", "mk", "mv", "Wr_b", "Wk_b", "Wv_b"]
    cols = [a["L0_attn_" + n].reshape(P) for n in names] + [a["L0_attn_u"].reshape(P), a["L0_attn_w"].reshape(P)]
    cols += list(a["L1_ffn_b1"]) + list(a["L1_ffn_b2"]) + [a["L0_attn_Wg_b"]]
    idx = _np.arange(P)
    same_head = (idx[:, None] // HD == idx[None, :] // HD).astype(_np.float32)
    eye = _np.eye(P, dtype=_np.float32)
    below = (idx[:, None] < idx[None, :]).astype(_np.float32)
    steps = _np.arange(E, dtype=_np.float32)
    ntl = -(-(x.shape[0] * x.shape[1] // P + E - 1) // NU) * NU
    w1b = _np.concatenate([a["L0_ffn_W1"], a["L0_ffn_b1"].reshape(E, FC, P).transpose(0, 2, 1)], axis=2)
    arrays = {
        "x": c(x.reshape(-1, P)),
        "w4": c(_np.stack([a[f"L0_attn_W{n}_w"].T for n in "grkv"], axis=1)),
        "wo": c(a["L0_attn_Wo_w"].T),
        "w1b": c(_np.concatenate([w1b, w1b[:1]])),
        "w2": c(a["L0_ffn_W2"]),
        "wqkv": c(a["L1_attn_Wqkv"].T),
        "wproj": c(a["L1_attn_Wproj"].T),
        "gate": c(a["L1_ffn_gate_w"].T),
        "l1": c(a["L1_ffn_w1"]), "l2": c(a["L1_ffn_w2"]), "l3": c(a["L1_ffn_w3"]),
        "cols": c(_np.stack(cols, axis=1)),
        "rows": c(_np.concatenate([a["L0_attn_Wo_b"], a["L1_attn_bproj"], a["L1_ffn_gate_b"], steps, E - steps,
                                   _np.arange(ntl, dtype=_np.float32)])),
        "b2": c(_np.concatenate([a["L0_ffn_b2"], a["L0_ffn_b2"][:1]])), "b3": c(a["L1_ffn_b3"]),
        "consts": _np.stack([eye, eye - same_head / HD, below]).astype(_np.float32),
    }
    nc = _bacc.Bacc("TRN2", target_bir_lowering=False, num_devices=1)
    args = [nc.dram_tensor("in_" + n, v.shape, _mybir.dt.from_np(v.dtype), kind="ExternalInput").ap() for n, v in arrays.items()]
    out = nc.dram_tensor("out_0", arrays["x"].shape, _mybir.dt.float32, kind="ExternalOutput").ap()
    two_layers(nc, *args, out)
    r = _run(nc, [{"in_" + n: v for n, v in arrays.items()}], core_ids=[0])
    return r.results[0]["out_0"].reshape(x.shape)
```
